# Optimizing a Trainium2 kernel written in Bass

```python
import numpy as np
import jax
import jax.numpy as jnp

def _softmax(x, axis=-1):
    return jax.nn.softmax(x, axis=axis)

def _gelu(x):
    return jax.nn.gelu(x, approximate=True)

def _silu(x):
    return jax.nn.silu(x)

def _sigmoid(x):
    return jax.nn.sigmoid(x)

def _layernorm(x, axis=-1, eps=1e-05):
    m = jnp.mean(x, axis=axis, keepdims=True)
    v = jnp.var(x, axis=axis, keepdims=True)
    return (x - m) / jnp.sqrt(v + eps)

def _scatter_add(tgt, idx, src, axis=0):
    return tgt.at[idx].add(src)

def _segment_sum(src, seg, n):
    return jax.ops.segment_sum(src, seg, n)
kernel_name = 'mk_sandwich_d1_jaxref_r8_0d72cb'

def setup_inputs(seed: int=0):
    np.random.seed(seed)
    _w = jnp.asarray

    def _L0_attn_setup():
        import jax, jax.numpy as jnp
        import numpy as np
        HEADS = 16
        DIM_HEAD = 64
        key = jax.random.key(seed)
        ks = jax.random.split(key, 5)
        b, n, dim = (4, 256, 128)
        return {'x': jax.random.normal(ks[0], (b, n, dim), dtype=jnp.float32), 'Wq': jax.random.normal(ks[1], (dim, HEADS * DIM_HEAD), dtype=jnp.float32) * dim ** (-0.5), 'Wkv': jax.random.normal(ks[2], (dim, DIM_HEAD), dtype=jnp.float32) * dim ** (-0.5), 'null_kv': jax.random.normal(ks[3], (DIM_HEAD,), dtype=jnp.float32), 'Wout': jax.random.normal(ks[4], (HEADS * DIM_HEAD, dim), dtype=jnp.float32) * (HEADS * DIM_HEAD) ** (-0.5)}
    _L0_attn_in = _L0_attn_setup()

    def _L0_ffn_setup():
        import jax, jax.numpy as jnp
        import numpy as np
        DIM = 128
        HIDDEN = 512
        E = 8
        K = 2

        def _ffn_hidden(h, multiple_of=32):
            h = int(2 * h / 3)
            return multiple_of * ((h + multiple_of - 1) // multiple_of)
        EXP_HID = _ffn_hidden(HIDDEN)
        SH_HID = _ffn_hidden(HIDDEN // 2)

        def _swiglu(t, a, b, c):
            return jax.nn.silu(t @ a) * (t @ c) @ b
        key = jax.random.key(seed)
        ks = jax.random.split(key, 8)

        def xavier(k, shape, fan_in, fan_out):
            lim = np.sqrt(6.0 / (fan_in + fan_out)).astype(np.float32)
            return jax.random.uniform(k, shape, jnp.float32, -lim, lim)
        return {'x': jax.random.normal(ks[0], (2, 256, DIM), jnp.float32), 'gate_w': xavier(ks[1], (E, DIM), DIM, E), 'w1': xavier(ks[2], (E, DIM, EXP_HID), DIM, EXP_HID), 'w2': xavier(ks[3], (E, EXP_HID, DIM), EXP_HID, DIM), 'w3': xavier(ks[4], (E, DIM, EXP_HID), DIM, EXP_HID), 'sw1': xavier(ks[5], (DIM, SH_HID), DIM, SH_HID), 'sw2': xavier(ks[6], (SH_HID, DIM), SH_HID, DIM), 'sw3': xavier(ks[7], (DIM, SH_HID), DIM, SH_HID)}
    _L0_ffn_in = _L0_ffn_setup()
    _d = {'L0_attn_x': _L0_attn_in['x'], 'L0_attn_Wq': _L0_attn_in['Wq'], 'L0_attn_Wkv': _L0_attn_in['Wkv'], 'L0_attn_null_kv': _L0_attn_in['null_kv'], 'L0_attn_Wout': _L0_attn_in['Wout'], 'L0_ffn_gate_w': _L0_ffn_in['gate_w'], 'L0_ffn_w1': _L0_ffn_in['w1'], 'L0_ffn_w2': _L0_ffn_in['w2'], 'L0_ffn_w3': _L0_ffn_in['w3'], 'L0_ffn_sw1': _L0_ffn_in['sw1'], 'L0_ffn_sw2': _L0_ffn_in['sw2'], 'L0_ffn_sw3': _L0_ffn_in['sw3']}
    _x0 = _d['L0_attn_x']
    _d['L0_attn_x'] = jax.random.normal(jax.random.fold_in(jax.random.key(seed), 1), (2, 1024, 128), dtype=_x0.dtype)
    del _x0
    return _d

def reference(L0_attn_x, L0_attn_Wq, L0_attn_Wkv, L0_attn_null_kv, L0_attn_Wout, L0_ffn_gate_w, L0_ffn_w1, L0_ffn_w2, L0_ffn_w3, L0_ffn_sw1, L0_ffn_sw2, L0_ffn_sw3):

    def _L0_attn_ref(x, Wq, Wkv, null_kv, Wout):
        import jax, jax.numpy as jnp
        import numpy as np
        HEADS = 16
        DIM_HEAD = 64
        b, n, dim = x.shape
        scale = DIM_HEAD ** (-0.5)
        q = (x @ Wq).reshape(b, n, HEADS, DIM_HEAD).transpose(0, 2, 1, 3) * scale
        kv = x @ Wkv
        kv = jnp.concatenate([jnp.broadcast_to(null_kv, (b, 1, DIM_HEAD)), kv], axis=1)
        sim = jnp.einsum('bhid,bjd->bhij', q, kv)
        mask_value = -jnp.finfo(sim.dtype).max
        i, j = (sim.shape[-2], sim.shape[-1])
        causal_mask = jnp.triu(jnp.ones((i, j), dtype=bool), k=j - i + 1)
        sim = jnp.where(causal_mask, mask_value, sim)
        attn = jax.nn.softmax(sim.astype(jnp.float32), axis=-1)
        out = jnp.einsum('bhij,bjd->bhid', attn, kv.astype(jnp.float32))
        out = out.transpose(0, 2, 1, 3).reshape(b, n, HEADS * DIM_HEAD)
        return out @ Wout

    def _L0_ffn_ref(x, gate_w, w1, w2, w3, sw1, sw2, sw3):
        import jax, jax.numpy as jnp
        import numpy as np
        DIM = 128
        HIDDEN = 512
        E = 8
        K = 2

        def _ffn_hidden(h, multiple_of=32):
            h = int(2 * h / 3)
            return multiple_of * ((h + multiple_of - 1) // multiple_of)
        EXP_HID = _ffn_hidden(HIDDEN)
        SH_HID = _ffn_hidden(HIDDEN // 2)

        def _swiglu(t, a, b, c):
            return jax.nn.silu(t @ a) * (t @ c) @ b
        B, S, D = x.shape
        xt = x.reshape(-1, D)
        T = xt.shape[0]
        logits = xt @ gate_w.T
        scores = jax.nn.softmax(logits, axis=-1)
        topk_w, topk_i = jax.lax.top_k(scores, K)
        comb = jnp.zeros((T, E), x.dtype).at[jnp.arange(T)[:, None], topk_i].add(topk_w)
        y = jnp.zeros_like(xt)
        for e in range(E):
            y = y + comb[:, e:e + 1] * _swiglu(xt, w1[e], w2[e], w3[e])
        y = y.reshape(B, S, D)
        return y + _swiglu(x, sw1, sw2, sw3)
    x = L0_attn_x
    x = x + _layernorm(_L0_attn_ref(_layernorm(x, axis=-1), L0_attn_Wq, L0_attn_Wkv, L0_attn_null_kv, L0_attn_Wout), axis=-1)
    x = x + _layernorm(_L0_ffn_ref(_layernorm(x, axis=-1), L0_ffn_gate_w, L0_ffn_w1, L0_ffn_w2, L0_ffn_w3, L0_ffn_sw1, L0_ffn_sw2, L0_ffn_sw3), axis=-1)
    return x

_drawn_inputs = setup_inputs


def setup_inputs(seed=0):
    import zlib

    import numpy as np

    out = dict(_drawn_inputs(seed))
    spreads = {}
    factors = {}
    for name, (base, spread) in spreads.items():
        noise = np.random.default_rng([zlib.crc32(name.encode()), seed]).standard_normal(out[name].shape)
        drawn = base * np.exp(spread * noise) if base else spread * noise
        out[name] = jnp.asarray(drawn.astype(out[name].dtype))
    for name, factor in factors.items():
        out[name] = (out[name] * factor).astype(out[name].dtype)
    return out
```

```python
from contextlib import ExitStack

import numpy as np

import concourse.bass as bass
from concourse import mybir

F32 = mybir.dt.float32
F32R = mybir.dt.float32r
BF16 = mybir.dt.bfloat16
ALU = mybir.AluOpType
ACT = mybir.ActivationFunctionType
AX_X = mybir.AxisListType.X

P = 128
CH = 512
EPS = 1e-5
MASKED = -1.0e38
LOWEST = -3.0e38


def sandwich_layer(nc, x, wq, wkv, null_kv, wout, gate_w, w1, w2, w3, sw1, sw2, sw3, ident_f, ident_b,
                   mask_t, mask_n, mask_fix, out):
    B, N, D = x.shape
    DH = null_kv.shape[0]
    HEADS = wq.shape[1] // DH
    PAIRS = HEADS // 2
    TOK = B * N
    NT = TOK // P
    NB = N // P
    NCH = N // CH
    BPC = CH // P
    E, _, HID = w1.shape
    SHID = sw1.shape[1]
    SCALE = float(DH) ** -0.5
    assert D == P and DH == 64 and N == 1024 and NCH == 2
    assert HID > 2 * P and HID <= 3 * P and SHID > P and SHID <= 2 * P

    tiles = [None]
    for c in range(NCH):
        for kb in range(BPC * (c + 1)):
            first = P * kb - 2 - CH * c if P * kb - 1 > CH * c else 0
            tiles.append((c, kb, first))
    T = len(tiles)
    TF = T - 1
    last_of = [max(t for t in range(1, T) if tiles[t][0] == c) for c in range(NCH)]
    first_of = [min(t for t in range(1, T) if tiles[t][0] == c) for c in range(NCH)]

    units = [(qb, kc, min(P * (qb + 1) - CH * kc, CH)) for qb in range(NB) for kc in range(qb // BPC + 1)]
    U = len(units)
    NPB = 3

    with ExitStack() as ctx:
        def sb(name, shape, dt=F32):
            return ctx.enter_context(nc.sbuf_tensor(name, shape, dt))

        def sem(name):
            return ctx.enter_context(nc.semaphore(name))

        x_sb = sb("x_sb", [P, NT, D])
        xn = sb("xn", [P, NT, D])
        xt_hi = sb("xt_hi", [P, TOK], F32R)
        xt_lo = sb("xt_lo", [P, TOK], F32R)
        stats = sb("stats", [P, NT, 6])
        mv = sb("mv", [P, NT, 2])
        vare = sb("vare", [P, NT])
        std = sb("std", [P, NT])
        rstd = sb("rstd", [P, NT])
        attn = sb("attn", [P, NT, D])
        ident = sb("ident", [P, P])
        neg_ident = sb("neg_ident", [P, P])
        identb = sb("identb", [P, P], BF16)
        maskt = sb("maskt", [P, P + 2], BF16)
        maskn = sb("maskn", [P, P], BF16)
        maskf = sb("maskf", [2, 2], BF16)
        ones = sb("ones", [P, DH])
        row_sel = sb("row_sel", [P, DH + 1], F32R)
        wq_hi = sb("wq_hi", [P, HEADS * DH + P], F32R)
        wq_lo = sb("wq_lo", [P, HEADS * DH + P], F32R)
        wcur_hi = sb("wcur_hi", [P, 2, 2, DH], F32R)
        wcur_lo = sb("wcur_lo", [P, 2, 2, DH], F32R)
        wkv_raw = sb("wkv_raw", [P, 2, DH])
        wkv_hi = sb("wkv_hi", [P, 2, DH], F32R)
        wkv_lo = sb("wkv_lo", [P, 2, DH], F32R)
        null_bc = sb("null_bc", [P, DH])
        null_col = sb("null_col", [P, 1])
        wn = sb("wn", [P, HEADS])
        wn_hi = sb("wn_hi", [P, HEADS], F32R)
        wn_lo = sb("wn_lo", [P, HEADS], F32R)
        s_null = sb("s_null", [P, NT, HEADS])
        kf_room = sb("kf_room", [P, B * (N + 2)])
        kf = kf_room[0:DH, :].rearrange("p (b n) -> p b n", b=B)
        k_hi = sb("k_hi", [P, B, N + 2], F32R)
        k_lo = sb("k_lo", [DH + 1, B, N + 2], F32R)
        v_sb = sb("v_sb", [P, B, NB, DH])
        v_fix = sb("v_fix", [2, B, DH])
        q_split = sb("q_split", [P, 2, 2, N], F32R)
        q_hi = sb("q_hi", [P, 2, 2, N], F32R)
        probs = sb("probs", [P, NPB, 2, CH])
        probs_fix = sb("probs_fix", [2, 2, 2, 2])
        psums = sb("psums", [P, NCH, 2, CH])
        wn_prod = psums[:].rearrange("p c h n -> p (c h n)")[:, 0:HEADS * DH].rearrange("p (h d) -> p h d", d=DH)
        m_part = sb("m_part", [P, 2, NB, 2])
        m_real = sb("m_real", [P, 2, NB])
        m_all = sb("m_all", [P, 2, NB])
        spread = sb("spread", [P, 2, NB, P], F32R)
        inv = sb("inv", [P, NCH, CH])
        heads_out = sb("heads_out", [P, PAIRS, N])
        wq_raw = heads_out[:, 0, 0:HEADS * DH]
        wout_sb = sb("wout_sb", [P, PAIRS, D])

        gate_raw = sb("gate_raw", [E, D])
        gate_t = sb("gate_t", [P, E])
        gate_hi = sb("gate_hi", [P, E], F32R)
        gate_lo = sb("gate_lo", [P, E], F32R)
        logits = sb("logits", [P, NT, E])
        top = sb("top", [P, NT, 8])
        rest = sb("rest", [P, NT, E])
        low = sb("low", [P, NT])
        comb = sb("comb", [P, NT, E])
        up_raw = kf_room[:, 0:4 * HID].rearrange("p (k m n) -> p k m n", k=2, m=2)
        up_hi = sb("up_hi", [P, 2, 2, HID], F32R)
        up_lo = sb("up_lo", [P, 2, 2, HID], F32R)
        down_w = sb("down_w", [P, 2, 3, D])
        gated = probs[:, 0, :, :]
        hidden = heads_out[:].rearrange("p a n -> p (a n)")[:, 0:6 * CH].rearrange("p (j i n) -> p j i n", j=2, i=3)

        scores = ctx.enter_context(nc.psum_tensor("scores", [P, 2, 2, CH], F32))
        o_ps = ctx.enter_context(nc.psum_tensor("o_ps", [P, NCH, CH], F32))
        misc = ctx.enter_context(nc.psum_tensor("misc", [P, 2, CH], F32))

        x_loaded = [sem(f"x_loaded{q}") for q in range(NT // 4)]
        c_loaded, w_loaded = sem("c_loaded"), sem("w_loaded")
        vec = sem("vec")
        var_ready, sqrt_done = sem("var_ready"), sem("sqrt_done")
        norm_done = sem("norm_done")
        turned = sem("turned")
        t_high, t_low = sem("t_high"), sem("t_low")
        consts_ready = sem("consts_ready")
        wsplit = sem("wsplit")
        kv_filled, kv_high, kv_copied, kv_low = sem("kv_filled"), sem("kv_high"), sem("kv_copied"), sem("kv_low")
        v_turned, v_copied = sem("v_turned"), sem("v_copied")
        null_filled, null_copied = sem("null_filled"), sem("null_copied")
        wcur_ready = sem("wcur_ready")
        q_filled, q_high, q_low, q_copied = sem("q_filled"), sem("q_high"), sem("q_low"), sem("q_copied")
        unit_filled, unit_max, real_max, head_max = (sem("unit_filled"), sem("unit_max"), sem("real_max"),
                                                     sem("head_max"))
        spread_ready, row_filled, row_copied = sem("spread_ready"), sem("row_filled"), sem("row_copied")
        scores_ready, probs_ready, av_done = sem("scores_ready"), sem("probs_ready"), sem("av_done")
        summed, sums_ready = sem("summed"), sem("sums_ready")
        den_filled, inv_ready, o_done = sem("den_filled"), sem("inv_ready"), sem("o_done")
        proj_filled, proj_copied = sem("proj_filled"), sem("proj_copied")
        stored = sem("stored")
        g_loaded, gate_turned, gate_split = sem("g_loaded"), sem("gate_turned"), sem("gate_split")
        logits_filled, logits_copied, exp_done = sem("logits_filled"), sem("logits_copied"), sem("exp_done")
        ew_loaded = [sem(f"ew_loaded{k}") for k in range(2)]
        ew_high, ew_split = sem("ew_high"), sem("ew_split")
        up_filled, silu_done, hidden_ready = sem("up_filled"), sem("silu_done"), sem("hidden_ready")
        down_filled, added = sem("down_filled"), sem("added")
        result_ready = sem("result_ready")
        block = ctx.enter_context(nc.Block())

        UNIT_STEPS = {3: 3, 4: 2, 5: 2, 6: 3, 7: 2, 8: 3, 9: 2, 10: 3, 11: 2, 12: 2}
        assert sum(UNIT_STEPS.values()) == 2 * U
        DEN0_STEP = 8

        def misc_uses(prev, nxt, proj):
            uses = []
            if nxt:
                uses += [("q", 1, i) for i in range(2 * NCH)]
            if prev:
                uses += [("den", -1, 1)]
            uses += [("row", 0, i) for i in range(2 * NCH)]
            if proj:
                uses += [("proj", 0, i) for i in range(NB)]
            n = 0
            for t in range(1, T):
                if t == DEN0_STEP:
                    uses.append(("den", 0, 0))
                if nxt:
                    for _ in range(UNIT_STEPS.get(t, 0)):
                        uses.append(("unit", 1, n))
                        n += 1
            return uses

        PER_PAIR = {"q": 2 * NCH, "row": 2 * NCH, "unit": 2 * U, "den": NCH}
        READ_BY = {"q": q_low, "row": row_copied, "unit": unit_max, "den": inv_ready, "proj": proj_copied}

        def plan(g):
            return dict(prev=g > 0, nxt=g < B * PAIRS - 1, proj=g == PAIRS)

        def uses_of(g):
            if g < 0:
                return [("q", 1, i) for i in range(2 * NCH)] + [("unit", 1, i) for i in range(2 * U)]
            return misc_uses(**plan(g))

        def banks_of(g):
            start = 0
            for k in range(-1, g):
                start += len(uses_of(k))
            return {u: (start + n) % 2 for n, u in enumerate(uses_of(g))}

        def all_pairs(eng, body):
            for b in range(B):
                body(b * PAIRS, b * PAIRS, b)
                with eng.Fori(0, (PAIRS - 2) // 2) as i:
                    for k in (1, 2):
                        body(2 * i + (b * PAIRS + k), b * PAIRS + 2 + k, b)
                body((b + 1) * PAIRS - 1, (b + 1) * PAIRS - 1, b)

        NJ = TOK // CH
        pieces = [(0, P), (P, P), (2 * P, HID - 2 * P)]
        shared_pieces = [(0, P), (P, SHID - P)]
        E_LOADS = 16 * 4

        def pieces_of(s):
            return pieces if s else shared_pieces

        def units_before(number):
            return len(shared_pieces) * NJ + len(pieces) * NJ * (number - 1) if not isinstance(number, int) or number \
                else 0

        def all_experts(eng, body):
            for s in range(3):
                body(s, s)
            with eng.Fori(0, (E - 2) // 2) as i:
                for k in (3, 4):
                    body(2 * i + k, k)

        @block.sync
        def _(sp):
            for t0 in range(0, NT, 4):
                sp.dma_start(x_sb[:, t0:t0 + 4, :],
                             x.rearrange("b n d -> (b n) d").rearrange("(t p) d -> p t d", p=P)[:, t0:t0 + 4, :]
                             ).then_inc(x_loaded[t0 // 4], 16)
            for dst, src in ((ident, ident_f), (identb, ident_b), (maskt, mask_t), (maskn, mask_n), (maskf, mask_fix)):
                sp.dma_start(dst[:], src).then_inc(c_loaded, 16)
            sp.dma_start(wq_raw, wq).then_inc(w_loaded, 16)
            for j in range(2):
                sp.dma_start(wkv_raw[:, j, :], wkv).then_inc(w_loaded, 16)
                sp.dma_start(null_col[j * DH:(j + 1) * DH, :], null_kv.rearrange("(d a) -> d a", a=1)
                             ).then_inc(w_loaded, 16)
            for b in range(B):
                sp.dma_start(kf[:, b, 0:1], null_kv.rearrange("(d a) -> d a", a=1)).then_inc(w_loaded, 16)
            sp.dma_start(null_bc[:], null_kv.rearrange("(a d) -> a d", a=1).broadcast_to([P, DH])
                         ).then_inc(w_loaded, 16)
            sp.dma_start(wout_sb[:], wout.rearrange("(p k) n -> k p n", k=P)).then_inc(w_loaded, 16)
            sp.dma_start(gate_raw[:], gate_w).then_inc(g_loaded, 16)

            sp.wait_ge(v_turned, B + 1)
            sp.wait_ge(kv_low, B * NCH + B)

            def body(number, s):
                k = s % 2
                if s >= 2:
                    sp.wait_ge(down_filled, NJ * (number - 1))
                if s == 0:
                    srcs, hid = (sw1, sw3, sw2), SHID
                else:
                    e = number - 1
                    srcs = tuple(w[bass.ds(e, 1), :, :].rearrange("o a b -> (o a) b") for w in (w1, w3, w2))
                    hid = HID
                for j in range(2):
                    sp.dma_start(up_raw[:, k, j, 0:hid], srcs[j]).then_inc(ew_loaded[k], 16)
                whole = hid // P
                sp.dma_start(down_w[:, k, 0:whole, :],
                             srcs[2][0:whole * P, :].rearrange("(c p) d -> p c d", p=P)).then_inc(ew_loaded[k], 16)
                sp.dma_start(down_w[0:hid - whole * P, k, whole, :], srcs[2][whole * P:hid, :]
                             ).then_inc(ew_loaded[k], 16)

            all_experts(sp, body)
            for q in range(4):
                sp.wait_ge(result_ready, q + 1)
                sp.dma_start(out.rearrange("b n d -> (b n) d").rearrange("(t p) d -> p t d", p=P)[:, 4 * q:4 * q + 4, :],
                             xn[:, 4 * q:4 * q + 4, :]).then_inc(stored, 16)
            sp.wait_ge(stored, 16 * 4)

        W_LOADS = 16 * (1 + 4 + B + 2)

        @block.gpsimd
        def _(pool):
            pool.memset(ones[:], 1.0)
            pool.memset(m_part[:], LOWEST)
            pool.memset(row_sel[:, 0:DH].bitcast(F32), 0.0)
            pool.memset(row_sel[:, DH:DH + 1].bitcast(F32), 1.0).then_inc(consts_ready, 1)

            def body(number, g, b):
                for t in range(1, T):
                    c, kb, first = tiles[t]
                    t0 = first_of[c]
                    slot = (t - 1) % NPB
                    if t == t0:
                        continue
                    pool.wait_ge(probs_ready, T * number + t + 1)
                    acc = psums[:, c, :, :]
                    if t == t0 + 1:
                        if g > 0:
                            pool.wait_ge(den_filled, NCH * (number - 1) + c + 1)
                        before = probs[:, (t0 - 1) % NPB, :, :]
                        pool.tensor_tensor(acc[:, :, first:CH], before[:, :, first:CH], probs[:, slot, :, first:CH],
                                           ALU.add).then_inc(summed, 1 if first else 2)
                        if first:
                            pool.tensor_scalar(acc[:, :, 0:first], before[:, :, 0:first], 1.0, None, ALU.mult
                                               ).then_inc(summed, 1)
                    else:
                        pool.wait_ge(summed, TF * number + t - 1)
                        pool.tensor_tensor(acc[:, :, first:CH], acc[:, :, first:CH], probs[:, slot, :, first:CH],
                                           ALU.add).then_inc(summed, 1)
                    if t == last_of[c]:
                        pool.wait_ge(summed, TF * number + t)
                        pool.tensor_tensor(acc[0:2, :, CH - 1], acc[0:2, :, CH - 1], probs_fix[:, g % 2, :, c],
                                           ALU.add).then_inc(sums_ready, 1)

            all_pairs(pool, body)

            def split_weights(number, s):
                k, hid = s % 2, HID if s else SHID
                pool.wait_ge(ew_loaded[k], (number - k) * (E_LOADS // 2) + E_LOADS)
                if s >= 2:
                    pool.wait_ge(up_filled, units_before(number - 1))
                pool.tensor_tensor(up_hi[:, k, :, 0:hid], up_raw[:, k, :, 0:hid],
                                   ones[:, 0:1].unsqueeze(2).broadcast_to([P, 2, hid]), ALU.mult).then_inc(ew_high, 1)
                pool.wait_ge(ew_high, number + 1)
                pool.tensor_tensor(up_lo[:, k, :, 0:hid], up_raw[:, k, :, 0:hid], up_hi[:, k, :, 0:hid].bitcast(F32),
                                   ALU.subtract).then_inc(ew_split, 1)

            all_experts(pool, split_weights)

        @block.scalar
        def _(act):
            act.wait_ge(var_ready, 1)
            act.activation(std[:], vare[:], ACT.Sqrt).then_inc(sqrt_done, 1)
            for j in range(NT // 4):
                act.wait_ge(turned, j + 1)
                act.activation(xt_hi[:, j * CH:(j + 1) * CH], scores[:, j // 2 % 2, j % 2, :], ACT.Copy
                               ).then_inc(t_high, 1)
            for j in range(B * NCH):
                b, c = divmod(j, NCH)
                act.wait_ge(kv_filled, j + 1)
                act.activation(k_hi[:, b, 1 + c * CH:1 + (c + 1) * CH], scores[:, j // 2 % 2, j % 2, :], ACT.Copy
                               ).then_inc(kv_high, 1)
            act.wait_ge(w_loaded, W_LOADS)
            for b in range(B):
                act.activation(k_hi[:, b, 0:1], null_col[:], ACT.Copy).then_inc(kv_high, 1)
            for b in range(B):
                act.wait_ge(v_turned, b + 1)
                act.activation(v_sb[:, b, :, :], o_ps[:, b, :].rearrange("p (k d) -> p k d", d=DH), ACT.Copy
                               ).then_inc(v_copied, 1)
            act.wait_ge(v_turned, B + 1)
            act.activation(v_fix[:], misc[0:2, 1, 0:B * DH].rearrange("p (b d) -> p b d", b=B), ACT.Copy
                           ).then_inc(v_copied, 1)
            act.wait_ge(null_filled, 1)
            act.activation(s_null[:], misc[:, 0, 0:NT * HEADS].rearrange("p (t h) -> p t h", h=HEADS), ACT.Copy
                           ).then_inc(null_copied, 1)

            def weights(pair):
                for dst, src in ((wcur_hi, wq_hi), (wcur_lo, wq_lo)):
                    for j in range(2):
                        act.activation(dst[:, :, j, :],
                                       src[:, bass.ds(pair * P, P)].bitcast(F32).rearrange("p (h d) -> p h d", h=2),
                                       ACT.Copy).then_inc(wcur_ready, 1)

            def high_parts(number, g):
                par, banks = (g + 1) % 2, banks_of(g)
                for i in range(2 * NCH):
                    h, c = divmod(i, NCH)
                    act.wait_ge(q_filled, PER_PAIR["q"] * (number + 1) + i + 1)
                    if i == 0 and g >= 1:
                        act.wait_ge(scores_ready, T * number)
                    act.activation(q_split[0:DH, par, h, c * CH:(c + 1) * CH], misc[0:DH, banks["q", 1, i], :],
                                   ACT.Copy).then_inc(q_copied, 1)
                    act.activation(q_hi[:, par, h, c * CH:(c + 1) * CH], misc[:, banks["q", 1, i], :],
                                   ACT.Copy).then_inc(q_high, 1)

            act.wait_ge(wsplit, 4)
            weights(0)
            high_parts(-1, -1)
            weights(1)

            def body(number, g, b):
                todo = plan(g)
                if todo["nxt"]:
                    high_parts(number, g)
                    if g + 2 < B * PAIRS:
                        weights(number + 2 - b * PAIRS if g % PAIRS < PAIRS - 1 else 1)
                banks = banks_of(g)
                for i in range(2 * NCH):
                    h, c = divmod(i, NCH)
                    act.wait_ge(row_filled, PER_PAIR["row"] * number + i + 1)
                    act.activation(q_hi[DH:DH + 1, g % 2, h, c * CH:(c + 1) * CH], misc[DH:DH + 1, banks["row", 0, i], :],
                                   ACT.Copy).then_inc(row_copied, 1)
                for t in range(T):
                    st = (g * T + t) % 2
                    act.wait_ge(scores_ready, T * number + t + 1)
                    if t == 0:
                        act.activation(probs_fix[:, g % 2, :, :], scores[0:2, st, :, 0:2], ACT.Exp
                                       ).then_inc(probs_ready, 1)
                        continue
                    c, kb, first = tiles[t]
                    slot = (t - 1) % NPB
                    if t > NPB:
                        old = t - NPB
                        act.wait_ge(av_done, TF * number + old)
                        act.wait_ge(summed, TF * number + old + (1 if old in first_of else 0))
                    elif g > 0:
                        old = TF + t - NPB
                        act.wait_ge(av_done, TF * (number - 1) + old)
                        act.wait_ge(summed, TF * (number - 1) + old)
                    act.activation(probs[:, slot, :, first:CH], scores[:, st, :, first:CH], ACT.Exp
                                   ).then_inc(probs_ready, 1)
                    if t == 1 and todo["proj"]:
                        project_copies(0, banks)

            def project_copies(b, banks):
                for i in range(NB):
                    act.wait_ge(proj_filled, b * NB + i + 1)
                    bank = banks["proj", 0, i] if banks else i % 2
                    act.activation(attn[:, b * NB + i, :], misc[:, bank, 0:D], ACT.Copy).then_inc(proj_copied, 1)

            all_pairs(act, body)
            project_copies(B - 1, None)

            for n in (1, 2):
                act.wait_ge(var_ready, n + 1)
                act.activation(std[:], vare[:], ACT.Sqrt).then_inc(sqrt_done, 1)
            for j in range(NT // 4):
                act.wait_ge(turned, NT // 4 + j + 1)
                act.activation(xt_hi[:, j * CH:(j + 1) * CH], scores[:, j // 2 % 2, j % 2, :], ACT.Copy
                               ).then_inc(t_high, 1)
            act.wait_ge(logits_copied, 1)
            act.activation(rest[:], logits[:], ACT.Exp).then_inc(exp_done, 1)

            def silu(number, s):
                for j in range(NJ):
                    for i, (_, rows_) in enumerate(pieces_of(s)):
                        n = j * len(pieces_of(s)) + i
                        at = units_before(number) + n
                        act.wait_ge(up_filled, at + 1)
                        if s or n >= 2:
                            act.wait_ge(hidden_ready, at - 1)
                        act.activation(gated[0:rows_, n % 2, :], scores[0:rows_, n % 2, 0, :], ACT.Silu
                                       ).then_inc(silu_done, 1)

            all_experts(act, silu)
            act.wait_ge(var_ready, 4)
            act.activation(std[:], vare[:], ACT.Sqrt).then_inc(sqrt_done, 1)

        @block.tensor
        def _(pe):
            pe.wait_ge(c_loaded, 16 * 5)
            def turn_tokens(n):
                for t in range(NT):
                    j = t // 4
                    pe.wait_ge(norm_done, n * NT + t + 1)
                    mm = pe.transpose(scores[:, j // 2 % 2, j % 2, (t % 4) * P:(t % 4 + 1) * P], xn[:, t, :],
                                      ident[:])
                    if t % 4 == 3:
                        mm.then_inc(turned, 1)

            turn_tokens(0)
            pe.wait_ge(wsplit, 4)
            for j in range(B * NCH):
                pe.wait_ge(t_high, j + 1)
                pe.wait_ge(t_low, j + 1)
                dst = scores[:, j // 2 % 2, j % 2, :]
                sl = slice(j * CH, (j + 1) * CH)
                pe.matmul(dst, wkv_hi[:].rearrange("p a d -> p (a d)"), xt_hi[:, sl], start=True, stop=False)
                pe.matmul(dst, wkv_lo[:].rearrange("p a d -> p (a d)"), xt_hi[:, sl], start=False, stop=False)
                pe.matmul(dst, wkv_hi[:].rearrange("p a d -> p (a d)"), xt_lo[:, sl], start=False, stop=True
                          ).then_inc(kv_filled, 1)
            for t in range(NT):
                dst = misc[:, 0, t * HEADS:(t + 1) * HEADS]
                sl = slice(t * P, (t + 1) * P)
                pe.matmul(dst, xt_hi[:, sl], wn_hi[:], start=True, stop=False)
                pe.matmul(dst, xt_hi[:, sl], wn_lo[:], start=False, stop=False)
                mm = pe.matmul(dst, xt_lo[:, sl], wn_hi[:], start=False, stop=True)
            mm.then_inc(null_filled, 1)
            pe.wait_ge(kv_copied, B * NCH)
            for b in range(B):
                for kb in range(NB):
                    mm = pe.transpose(o_ps[:, b, kb * DH:(kb + 1) * DH], kf[:, b, kb * P:(kb + 1) * P],
                                      ident[0:DH, 0:DH])
                mm.then_inc(v_turned, 1)
            for b in range(B):
                mm = pe.transpose(misc[0:2, 1, b * DH:(b + 1) * DH], kf[:, b, CH:N + 1:CH], ident[0:DH, 0:DH])
            mm.then_inc(v_turned, 1)
            pe.wait_ge(null_copied, 1)
            pe.wait_ge(v_copied, B + 1)
            pe.wait_ge(kv_low, B * NCH + B)
            pe.wait_ge(kv_high, B * NCH + B)

            def take(g, number, kind, state):
                seq_before = uses_of(g - 1) if g >= 0 else []
                mine = uses_of(g)
                n = state[0]
                state[0] += 1
                assert mine[n][0] == kind, (mine[n], kind)
                seq = [(u, -1) for u in seq_before] + [(u, 0) for u in mine]
                at = len(seq_before) + n
                if at >= 2:
                    (k, rel, i), part = seq[at - 2]
                    if k == "proj":
                        pe.wait_ge(proj_copied, i + 1)
                    else:
                        pe.wait_ge(READ_BY[k], PER_PAIR[k] * (number + rel + part) + i + 1)
                return misc[:, banks_of(g)[mine[n]], :]

            def queries(g, number, state):
                nb = (g + 1) // PAIRS
                pe.wait_ge(wcur_ready, 4 * (number + 2))
                for i in range(2 * NCH):
                    h, c = divmod(i, NCH)
                    dst = take(g, number, "q", state)
                    sl = slice(nb * N + c * CH, nb * N + (c + 1) * CH)
                    hi = wcur_hi[:, h, :, :].rearrange("p a d -> p (a d)")
                    lo = wcur_lo[:, h, :, :].rearrange("p a d -> p (a d)")
                    pe.matmul(dst, hi, xt_hi[:, sl], start=True, stop=False)
                    pe.matmul(dst, hi, xt_lo[:, sl], start=False, stop=False)
                    pe.matmul(dst, lo, xt_hi[:, sl], start=False, stop=True).then_inc(q_filled, 1)

            def maximum_unit(g, number, i, state):
                nb, par = (g + 1) // PAIRS, (g + 1) % 2
                h, u = divmod(i, U)
                qb, kc, n = units[u]
                if u == 0:
                    pe.wait_ge(q_low, PER_PAIR["q"] * (number + 1) + NCH * (h + 1))
                    pe.wait_ge(q_copied, PER_PAIR["q"] * (number + 1) + NCH * (h + 1))
                dst = take(g, number, "unit", state)
                diagonal = kc == qb // BPC
                mm = pe.matmul(dst[:, 0:n], q_split[:, par, h, qb * P:(qb + 1) * P],
                               k_hi[:, nb, 1 + kc * CH:1 + kc * CH + n], start=True, stop=True)
                if diagonal:
                    mm = pe.matmul(dst[:, n - P:n], identb[:], maskn[:], start=False, stop=True,
                               skip_group_check=True)
                mm.then_inc(unit_filled, 1)

            def rows(g, number, state):
                for i in range(2 * NCH):
                    h, c = divmod(i, NCH)
                    pe.wait_ge(spread_ready, 2 * number + h + 1)
                    dst = take(g, number, "row", state)
                    pe.matmul(dst[0:DH + 1, :], row_sel[:],
                              spread[:, h, c * BPC:(c + 1) * BPC, :].rearrange("p b q -> p (b q)"),
                              start=True, stop=True).then_inc(row_filled, 1)

            def score(g, number, t, b):
                st, par = (g * T + t) % 2, g % 2
                use = T * number + t
                if t >= 2 or g > 0:
                    pe.wait_ge(probs_ready, use - 1)
                for h in range(2):
                    if t == 0:
                        qs = slice(CH - 1, N, CH)
                        ks = slice(CH, N + 1, CH)
                        dst = scores[0:2, st, h, 0:2]
                        pe.matmul(dst, k_hi[:, b, ks], q_split[:, par, h, qs], start=True, stop=False)
                        pe.matmul(dst, k_lo[:, b, ks], q_hi[0:DH + 1, par, h, qs], start=False, stop=False)
                        mm = pe.matmul(dst, identb[0:2, 0:2], maskf[:], start=False, stop=True)
                        continue
                    c, kb, first = tiles[t]
                    qs = slice(c * CH + first, (c + 1) * CH)
                    ks = slice(kb * P, (kb + 1) * P)
                    dst = scores[:, st, h, first:CH]
                    masked = kb * P - 2 + P > c * CH
                    pe.matmul(dst, k_hi[:, b, ks], q_split[:, par, h, qs], start=True, stop=False)
                    mm = pe.matmul(dst, k_lo[:, b, ks], q_hi[0:DH + 1, par, h, qs], start=False, stop=True)
                    if masked:
                        skip = 0 if first else 2
                        m0 = P * kb - 2 + skip - CH * c
                        w = P + 2 - skip
                        mm = pe.matmul(scores[:, st, h, m0:m0 + w], identb[:], maskt[:, skip:skip + w],
                                       start=False, stop=True, skip_group_check=True)
                mm.then_inc(scores_ready, 1)

            def weigh(g, number, t, b):
                c, kb, first = tiles[t]
                pe.wait_ge(probs_ready, T * number + t + 1)
                if t == first_of[c] and g > 0:
                    pe.wait_ge(o_done, NCH * (number - 1) + c + 1)
                slot = (t - 1) % NPB
                for h in range(2):
                    mm = pe.matmul(o_ps[h * DH:(h + 1) * DH, c, first:CH], v_sb[:, b, kb, :],
                                   probs[:, slot, h, first:CH], start=t == first_of[c], stop=t == last_of[c],
                                   skip_group_check=True)
                    if t == first_of[c]:
                        mm = pe.matmul(o_ps[h * DH:(h + 1) * DH, c, CH - 1:CH], v_fix[:, b, :],
                                       probs_fix[:, g % 2, h, c:c + 1], start=False, stop=False,
                                       skip_group_check=True)
                mm.then_inc(av_done, 1)

            def denominators(g, number, c, rel, state):
                pe.wait_ge(sums_ready, NCH * (number + rel) + c + 1)
                dst = take(g, number, "den", state)
                for h in range(2):
                    mm = pe.matmul(dst[h * DH:(h + 1) * DH, :], ones[:], psums[:, c, h, :], start=True, stop=True,
                                   skip_group_check=True)
                mm.then_inc(den_filled, 1)

            def project(b, g=None, number=None, state=None):
                pe.wait_ge(o_done, NCH * PAIRS * (b + 1))
                for i in range(NB):
                    if state is not None:
                        dst = take(g, number, "proj", state)
                    else:
                        dst = misc[:, i % 2, :]
                        if i < 2:
                            pe.wait_ge(inv_ready, NCH * PAIRS * B)
                        else:
                            pe.wait_ge(proj_copied, b * NB + i - 1)
                    for p in range(PAIRS):
                        mm = pe.matmul(dst[:, 0:D], heads_out[:, p, i * P:(i + 1) * P], wout_sb[:, p, :],
                                       start=p == 0, stop=p == PAIRS - 1)
                    mm.then_inc(proj_filled, 1)

            state = [0]
            queries(-1, -1, state)
            pe.wait_ge(consts_ready, 1)
            for i in range(2 * U):
                maximum_unit(-1, -1, i, state)

            def body(number, g, b):
                todo = plan(g)
                state = [0]
                if todo["nxt"]:
                    queries(g, number, state)
                if todo["prev"]:
                    denominators(g, number, 1, -1, state)
                rows(g, number, state)
                pe.wait_ge(row_copied, PER_PAIR["row"] * (number + 1))
                score(g, number, 0, b)
                score(g, number, 1, b)
                if todo["proj"]:
                    project(0, g, number, state)
                n = 0
                for t in range(1, T):
                    if t + 1 < T:
                        score(g, number, t + 1, b)
                    if t == DEN0_STEP:
                        denominators(g, number, 0, 0, state)
                    if todo["nxt"]:
                        for _ in range(UNIT_STEPS.get(t, 0)):
                            maximum_unit(g, number, n, state)
                            n += 1
                    weigh(g, number, t, b)
                if not todo["nxt"]:
                    pe.wait_ge(sums_ready, NCH * (number + 1))
                    pe.wait_ge(inv_ready, NCH * (number + 1) - 1)
                    for h in range(2):
                        mm = pe.matmul(misc[h * DH:(h + 1) * DH, 0, :], ones[:], psums[:, 1, h, :], start=True,
                                       stop=True, skip_group_check=True)
                    mm.then_inc(den_filled, 1)

            all_pairs(pe, body)
            project(B - 1)

            pe.wait_ge(g_loaded, 16)
            pe.wait_ge(proj_copied, NT)
            pe.transpose(misc[:, 0, 0:E], gate_raw[:], ident[0:E, 0:E]).then_inc(gate_turned, 1)
            pe.wait_ge(probs_ready, T * B * PAIRS)
            turn_tokens(1)
            pe.wait_ge(gate_split, 2)
            for t in range(NT):
                pe.wait_ge(t_low, NT // 4 + t // 4 + 1)
                sl = slice(t * P, (t + 1) * P)
                dst = misc[:, 1, t * E:(t + 1) * E]
                pe.matmul(dst, xt_hi[:, sl], gate_hi[:], start=True, stop=False)
                pe.matmul(dst, xt_hi[:, sl], gate_lo[:], start=False, stop=False)
                mm = pe.matmul(dst, xt_lo[:, sl], gate_hi[:], start=False, stop=True)
            mm.then_inc(logits_filled, 1)

            def up(number, s, j):
                k, sl = s % 2, slice(j * CH, (j + 1) * CH)
                for i, (r0, rows_) in enumerate(pieces_of(s)):
                    n = j * len(pieces_of(s)) + i
                    at = units_before(number) + n
                    if s or n >= 2:
                        pe.wait_ge(hidden_ready, at - 1)
                    for m in range(2):
                        dst = scores[0:rows_, n % 2, m, :]
                        hi, lo = up_hi[:, k, m, r0:r0 + rows_], up_lo[:, k, m, r0:r0 + rows_]
                        pe.matmul(dst, hi, xt_hi[:, sl], start=True, stop=False)
                        pe.matmul(dst, hi, xt_lo[:, sl], start=False, stop=False)
                        mm = pe.matmul(dst, lo, xt_hi[:, sl], start=False, stop=True)
                    mm.then_inc(up_filled, 1)

            def down(number, s, j):
                k, ps = s % 2, pieces_of(s)
                pe.wait_ge(hidden_ready, units_before(number) + (j + 1) * len(ps))
                if s or j >= 2:
                    pe.wait_ge(added, NJ * number + j - 1)
                for t in range(BPC):
                    for i, (_, rows_) in enumerate(ps):
                        mm = pe.matmul(o_ps[:, j % 2, t * P:(t + 1) * P], hidden[0:rows_, j % 2, i, t * P:(t + 1) * P],
                                       down_w[0:rows_, k, i, :], start=i == 0, stop=i == len(ps) - 1)
                mm.then_inc(down_filled, 1)

            def experts(number, s):
                pe.wait_ge(ew_split, number + 1)
                for j in range(NJ):
                    up(number, s, j)
                    if j:
                        down(number, s, j - 1)
                    elif s:
                        down(number - 1, 0 if s == 1 else s - 1, NJ - 1)

            all_experts(pe, experts)
            down(E, E, NJ - 1)

        @block.vector
        def _(dve):
            steps = [0]

            def link(ins):
                steps[0] += 1
                ins.then_inc(vec, 1)
                dve.wait_ge(vec, steps[0])

            def moments(n, src):
                for t in range(NT):
                    if n == 0 and t % 4 == 0:
                        dve.wait_ge(x_loaded[t // 4], 16)
                    if n == 1:
                        dve.wait_ge(proj_copied, t + 1)
                    done = dve.bn_stats(stats[:, t, :], src[:, t, :])
                link(done)
                for t in range(NT):
                    done = dve.bn_aggr(mv[:, t, :], stats[:, t, :])
                link(done)
                dve.tensor_scalar(vare[:], mv[:, :, 1], EPS, None, ALU.add).then_inc(var_ready, 1)
                dve.wait_ge(sqrt_done, n + 1)
                link(dve.reciprocal(rstd[:], std[:]))

            def normalize_tokens(src):
                for t in range(NT):
                    dve.tensor_scalar(xn[:, t, :], src[:, t, :], mv[:, t, 0:1], rstd[:, t:t + 1], ALU.subtract,
                                      ALU.mult).then_inc(norm_done, 1)

            def low_tokens(n):
                for j in range(NT // 4):
                    dve.wait_ge(t_high, n * (NT // 4) + j + 1)
                    dve.tensor_tensor(xt_lo[:, j * CH:(j + 1) * CH], scores[:, j // 2 % 2, j % 2, :],
                                      xt_hi[:, j * CH:(j + 1) * CH].bitcast(F32), ALU.subtract).then_inc(t_low, 1)

            moments(0, x_sb)
            normalize_tokens(x_sb)
            dve.wait_ge(w_loaded, W_LOADS)
            dve.wait_ge(c_loaded, 16 * 5)
            link(dve.tensor_scalar(wq_raw, wq_raw, SCALE, None, ALU.mult))
            WQ = HEADS * DH
            dve.tensor_copy(wq_hi[:, 0:WQ], wq_raw).then_inc(wsplit, 1)
            dve.tensor_copy(wkv_hi[:], wkv_raw[:]).then_inc(wsplit, 1)
            dve.wait_ge(wsplit, 2)
            dve.tensor_copy(wq_hi[:, WQ:WQ + P], wq_hi[:, 0:P].bitcast(F32))
            link(dve.tensor_tensor(wq_lo[:, 0:WQ], wq_raw, wq_hi[:, 0:WQ].bitcast(F32), ALU.subtract))
            dve.tensor_copy(wq_lo[:, WQ:WQ + P], wq_lo[:, 0:P].bitcast(F32)).then_inc(wsplit, 1)
            dve.tensor_tensor(wkv_lo[:], wkv_raw[:], wkv_hi[:].bitcast(F32), ALU.subtract)
            link(dve.tensor_tensor(wn_prod, wq_raw.rearrange("p (h d) -> p h d", d=DH),
                                   null_bc[:].unsqueeze(1).broadcast_to([P, HEADS, DH]), ALU.mult))
            link(dve.tensor_reduce(wn[:], wn_prod, AX_X, ALU.add))
            link(dve.tensor_copy(wn_hi[:], wn[:]))
            dve.tensor_scalar(neg_ident[:], ident[:], -1.0, None, ALU.mult)
            dve.tensor_tensor(wn_lo[:], wn[:], wn_hi[:].bitcast(F32), ALU.subtract).then_inc(wsplit, 1)
            low_tokens(0)
            for j in range(B * NCH):
                b, c = divmod(j, NCH)
                sl = slice(1 + c * CH, 1 + (c + 1) * CH)
                dve.wait_ge(kv_high, j + 1)
                dve.tensor_copy(kf[:, b, sl], scores[0:DH, j // 2 % 2, j % 2, :]).then_inc(kv_copied, 1)
                dve.tensor_tensor(k_lo[0:DH, b, sl], scores[0:DH, j // 2 % 2, j % 2, :],
                                  k_hi[0:DH, b, sl].bitcast(F32), ALU.subtract).then_inc(kv_low, 1)
            dve.memset(k_lo[DH:DH + 1, :, :].bitcast(F32), 1.0)
            dve.wait_ge(kv_high, B * NCH + B)
            for b in range(B):
                dve.tensor_tensor(k_lo[0:DH, b, 0:1], kf[:, b, 0:1], k_hi[0:DH, b, 0:1].bitcast(F32), ALU.subtract
                                  ).then_inc(kv_low, 1)

            def low_parts(g, number):
                par = (g + 1) % 2
                banks = banks_of(g)
                for i in range(2 * NCH):
                    h, c = divmod(i, NCH)
                    sl = slice(c * CH, (c + 1) * CH)
                    dve.wait_ge(q_high, PER_PAIR["q"] * (number + 1) + i + 1)
                    dve.tensor_tensor(q_split[DH:P, par, h, sl], misc[DH:P, banks["q", 1, i], :],
                                      q_hi[DH:P, par, h, sl].bitcast(F32), ALU.subtract).then_inc(q_low, 1)

            def unit(g, number, i):
                h, u = divmod(i, U)
                qb, kc, n = units[u]
                bank = banks_of(g)["unit", 1, i]
                dve.wait_ge(unit_filled, PER_PAIR["unit"] * (number + 1) + i + 1)
                dve.tensor_reduce(m_part[:, h, qb, kc:kc + 1], misc[:, bank, 0:n], AX_X, ALU.max
                                  ).then_inc(unit_max, 1)
                if u == U - 1:
                    whole_max(g, number, h)

            def whole_max(g, number, h):
                nb = (g + 1) // PAIRS
                head = 2 * (number + 1 - nb * PAIRS) + h
                dve.wait_ge(unit_max, PER_PAIR["unit"] * (number + 1) + (h + 1) * U)
                dve.tensor_reduce(m_real[:, h, :], m_part[:, h, :, :], AX_X, ALU.max).then_inc(real_max, 1)
                dve.wait_ge(real_max, 2 * (number + 1) + h + 1)
                dve.tensor_tensor(m_all[:, h, :], m_real[:, h, :],
                                  s_null[:, nb * NB:(nb + 1) * NB, bass.ds(head, 1)].rearrange("p t o -> p (t o)"),
                                  ALU.max).then_inc(head_max, 1)
                dve.wait_ge(head_max, 2 * (number + 1) + h + 1)
                if g >= 0:
                    dve.wait_ge(row_filled, PER_PAIR["row"] * number + NCH * (h + 1))
                dve.tensor_tensor(spread[:, h, :, :], neg_ident[:].unsqueeze(1).broadcast_to([P, NB, P]),
                                  m_all[:, h, :].unsqueeze(2).broadcast_to([P, NB, P]), ALU.mult
                                  ).then_inc(spread_ready, 1)

            def normalize(g, number, c, rel, bank):
                pair = number + rel - ((g + rel) // PAIRS) * PAIRS
                dve.wait_ge(den_filled, NCH * (number + rel) + c + 1)
                dve.reciprocal(inv[:, c, :], misc[:, bank, :]).then_inc(inv_ready, 1)
                dve.wait_ge(inv_ready, NCH * (number + rel) + c + 1)
                dve.wait_ge(av_done, TF * (number + rel) + last_of[c])
                if g == PAIRS and rel == 0:
                    dve.wait_ge(proj_filled, NB)
                dve.tensor_tensor(heads_out[:, bass.ds(pair, 1), c * CH:(c + 1) * CH].rearrange("p o n -> p (o n)"),
                                  o_ps[:, c, :], inv[:, c, :], ALU.mult).then_inc(o_done, 1)

            dve.wait_ge(null_copied, 1)
            dve.wait_ge(consts_ready, 1)
            low_parts(-1, -1)
            for i in range(2 * U):
                unit(-1, -1, i)

            def body(number, g, b):
                todo = plan(g)
                banks = banks_of(g)
                if todo["nxt"]:
                    low_parts(g, number)
                if todo["prev"]:
                    normalize(g, number, 1, -1, banks["den", -1, 1])
                n = 0
                for t in range(1, T):
                    if t == DEN0_STEP:
                        normalize(g, number, 0, 0, banks["den", 0, 0])
                    if todo["nxt"]:
                        for _ in range(UNIT_STEPS.get(t, 0)):
                            unit(g, number, n)
                            n += 1
                if not todo["nxt"]:
                    normalize(g, number, 1, 0, 0)

            all_pairs(dve, body)

            moments(1, attn)
            for t in range(NT):
                done = dve.tensor_scalar(xn[:, t, :], attn[:, t, :], mv[:, t, 0:1], rstd[:, t:t + 1], ALU.subtract,
                                         ALU.mult)
            link(done)
            link(dve.tensor_tensor(x_sb[:], x_sb[:], xn[:], ALU.add))
            moments(2, x_sb)
            normalize_tokens(x_sb)
            dve.wait_ge(gate_turned, 1)
            link(dve.tensor_copy(gate_t[:], misc[:, 0, 0:E]))
            dve.tensor_copy(gate_hi[:], gate_t[:]).then_inc(gate_split, 1)
            dve.wait_ge(gate_split, 1)
            dve.tensor_tensor(gate_lo[:], gate_t[:], gate_hi[:].bitcast(F32), ALU.subtract).then_inc(gate_split, 1)
            low_tokens(1)
            dve.wait_ge(logits_filled, 1)
            ps = misc[:, 1, 0:NT * E].rearrange("p (t e) -> p t e", e=E)
            link(dve.tensor_reduce(low[:], ps, AX_X, ALU.max))
            dve.tensor_tensor(logits[:], ps, low[:].unsqueeze(2).broadcast_to([P, NT, E]), ALU.subtract
                              ).then_inc(logits_copied, 1)
            dve.wait_ge(exp_done, 1)
            link(dve.tensor_reduce(low[:], rest[:], AX_X, ALU.add))
            link(dve.reciprocal(low[:], low[:]))
            link(dve.tensor_tensor(comb[:], rest[:], low[:].unsqueeze(2).broadcast_to([P, NT, E]), ALU.mult))
            for t in range(NT):
                done = dve.max(top[:, t, :], comb[:, t, :])
            link(done)
            link(dve.memset(top[:, :, 2:8], -1.0))
            for t in range(NT):
                done = dve.match_replace(rest[:, t, :], top[:, t, :], comb[:, t, :], 0.0)
            link(done)
            link(dve.tensor_tensor(comb[:], comb[:], rest[:], ALU.subtract))

            def products(number, s, j):
                for i, (_, rows_) in enumerate(pieces_of(s)):
                    n = j * len(pieces_of(s)) + i
                    at = units_before(number) + n
                    dve.wait_ge(silu_done, at + 1)
                    if i == 0 and (s or j >= 2):
                        dve.wait_ge(down_filled, NJ * number + j - 1)
                    dve.tensor_tensor(hidden[0:rows_, j % 2, i, :], gated[0:rows_, n % 2, :],
                                      scores[0:rows_, n % 2, 1, :], ALU.mult).then_inc(hidden_ready, 1)

            def add(number, s, j):
                dve.wait_ge(down_filled, NJ * number + j + 1)
                if s == 0:
                    dve.tensor_copy(attn[:, j * BPC:(j + 1) * BPC, :],
                                    o_ps[:, j % 2, :].rearrange("p (t d) -> p t d", d=D)).then_inc(added, 1)
                    return
                dve.wait_ge(added, NJ * (number - 1) + j + 1)
                for t in range(BPC):
                    tt = j * BPC + t
                    done = dve.scalar_tensor_tensor(out=attn[:, tt, :], in0=o_ps[:, j % 2, t * P:(t + 1) * P],
                                                    scalar=comb[:, tt, bass.ds(number - 1, 1)], in1=attn[:, tt, :],
                                                    op0=ALU.mult, op1=ALU.add)
                done.then_inc(added, 1)

            def experts(number, s):
                for j in range(NJ):
                    products(number, s, j)
                    if j:
                        add(number, s, j - 1)
                    elif s:
                        add(number - 1, s - 1, NJ - 1)

            all_experts(dve, experts)
            add(E, E, NJ - 1)

            dve.wait_ge(added, NJ * (E + 1))
            moments(3, attn)
            for t in range(NT):
                done = dve.tensor_scalar(attn[:, t, :], attn[:, t, :], mv[:, t, 0:1], rstd[:, t:t + 1], ALU.subtract,
                                         ALU.mult)
            link(done)
            for q in range(4):
                sl = slice(4 * q, 4 * q + 4)
                dve.tensor_tensor(xn[:, sl, :], x_sb[:, sl, :], attn[:, sl, :], ALU.add).then_inc(result_ready, 1)


_INS = ["L0_attn_x", "L0_attn_Wq", "L0_attn_Wkv", "L0_attn_null_kv", "L0_attn_Wout", "L0_ffn_gate_w", "L0_ffn_w1",
        "L0_ffn_w2", "L0_ffn_w3", "L0_ffn_sw1", "L0_ffn_sw2", "L0_ffn_sw3"]


def kernel(**inputs):
    import ml_dtypes
    import concourse.bacc as bacc
    from concourse.bass_utils import run_bass_kernel_spmd

    nc = bacc.Bacc("TRN2", target_bir_lowering=False, num_devices=1)
    arrays, args = {}, []

    def give(name, a):
        arrays[name] = a
        args.append(nc.dram_tensor(name, a.shape, mybir.dt.from_np(a.dtype), kind="ExternalInput").ap())

    for name in _INS:
        give(f"in_{name}_dram", np.ascontiguousarray(inputs[name]))
    bf16 = ml_dtypes.bfloat16
    give("ident_f", np.eye(P, dtype=np.float32))
    give("ident_b", np.eye(P, dtype=np.float32).astype(bf16))
    key, query = np.arange(P)[:, None], np.arange(-2, P)[None, :]
    give("mask_t", np.where(key > query + 1, MASKED, 0).astype(bf16))
    give("mask_n", np.where(np.arange(P)[None, :] > np.arange(P)[:, None], MASKED, 0).astype(bf16))
    give("mask_fix", np.where(np.eye(2) == 0, MASKED, 0).astype(bf16))
    shape = inputs["L0_attn_x"].shape
    args.append(nc.dram_tensor("out_0_dram", shape, F32, kind="ExternalOutput").ap())
    sandwich_layer(nc, *args)
    r = run_bass_kernel_spmd(nc, [arrays], core_ids=[0])
    return r.results[0]["out_0_dram"]
```

```python
from contextlib import ExitStack

import numpy as np

import concourse.bass as bass
from concourse import mybir

F32 = mybir.dt.float32
F32R = mybir.dt.float32r
BF16 = mybir.dt.bfloat16
ALU = mybir.AluOpType
ACT = mybir.ActivationFunctionType
AX_X = mybir.AxisListType.X

P = 128
CH = 512
EPS = 1e-5
MASKED = -1.0e38
LOWEST = -3.0e38


def sandwich_layer(nc, x, wq, wkv, null_kv, wout, gate_w, w1, w2, w3, sw1, sw2, sw3, ident_f, ident_b,
                   mask_t, mask_n, mask_fix, out):
    B, N, D = x.shape
    DH = null_kv.shape[0]
    HEADS = wq.shape[1] // DH
    PAIRS = HEADS // 2
    TOK = B * N
    NT = TOK // P
    NB = N // P
    NCH = N // CH
    BPC = CH // P
    E, _, HID = w1.shape
    SHID = sw1.shape[1]
    SCALE = float(DH) ** -0.5
    assert D == P and DH == 64 and N == 1024 and NCH == 2
    assert HID > 2 * P and HID <= 3 * P and SHID > P and SHID <= 2 * P

    tiles = [None]
    for c in range(NCH):
        for kb in range(BPC * (c + 1)):
            first = P * kb - 2 - CH * c if P * kb - 1 > CH * c else 0
            tiles.append((c, kb, first))
    T = len(tiles)
    TF = T - 1
    last_of = [max(t for t in range(1, T) if tiles[t][0] == c) for c in range(NCH)]
    first_of = [min(t for t in range(1, T) if tiles[t][0] == c) for c in range(NCH)]

    units = [(qb, kc, min(P * (qb + 1) - CH * kc, CH)) for qb in reversed(range(NB)) for kc in range(qb // BPC + 1)]
    U = len(units)
    NPB = 3
    NARROW = 2
    summed_after, SUMS = {}, 0
    for c in range(NCH):
        for t in range(first_of[c], last_of[c] - NARROW + 1):
            SUMS += 1
            summed_after[t] = SUMS
        summed_after[first_of[c]] += 1

    with ExitStack() as ctx:
        def sb(name, shape, dt=F32):
            return ctx.enter_context(nc.sbuf_tensor(name, shape, dt))

        def sem(name):
            return ctx.enter_context(nc.semaphore(name))

        x_sb = sb("x_sb", [P, NT, D])
        xn = sb("xn", [P, NT, D])
        xt_hi = sb("xt_hi", [P, TOK], F32R)
        xt_lo = sb("xt_lo", [P, TOK], F32R)
        stats = sb("stats", [P, NT, 6])
        mv = sb("mv", [P, NT, 2])
        vare = sb("vare", [P, NT])
        std = sb("std", [P, NT])
        rstd = sb("rstd", [P, NT])
        attn = sb("attn", [P, NT, D])
        ident = sb("ident", [P, P])
        neg_ident = sb("neg_ident", [P, P])
        identb = sb("identb", [P, P], BF16)
        maskt = sb("maskt", [P, P + 2], BF16)
        maskn = sb("maskn", [P, P], BF16)
        maskf = sb("maskf", [2, 2], BF16)
        ones = sb("ones", [P, DH])
        row_sel = sb("row_sel", [P, DH + 1], F32R)
        wq_hi = sb("wq_hi", [P, HEADS * DH + P], F32R)
        wq_lo = sb("wq_lo", [P, HEADS * DH + P], F32R)
        wcur_hi = sb("wcur_hi", [P, 2, 2, DH], F32R)
        wcur_lo = sb("wcur_lo", [P, 2, 2, DH], F32R)
        wkv_raw = sb("wkv_raw", [P, 2, DH])
        wkv_hi = sb("wkv_hi", [P, 2, DH], F32R)
        wkv_lo = sb("wkv_lo", [P, 2, DH], F32R)
        null_bc = sb("null_bc", [P, DH])
        null_col = sb("null_col", [P, 1])
        wn = sb("wn", [P, HEADS])
        wn_hi = sb("wn_hi", [P, HEADS], F32R)
        wn_lo = sb("wn_lo", [P, HEADS], F32R)
        s_null = sb("s_null", [P, NT, HEADS])
        kf_room = sb("kf_room", [P, B * (N + 2)])
        kf = kf_room[0:DH, :].rearrange("p (b n) -> p b n", b=B)
        k_hi = sb("k_hi", [P, B, N + 2], F32R)
        k_lo = sb("k_lo", [DH + 1, B, N + 2], F32R)
        v_sb = sb("v_sb", [P, B, NB, DH])
        v_fix = sb("v_fix", [2, B, DH])
        q_split = sb("q_split", [P, 2, 2, N], F32R)
        q_hi = sb("q_hi", [P, 2, 2, N], F32R)
        probs = sb("probs", [P, NPB, 2, CH])
        probs_fix = sb("probs_fix", [2, 2, 2, 2])
        psums = sb("psums", [P, NCH, 2, CH])
        wn_prod = psums[:].rearrange("p c h n -> p (c h n)")[:, 0:HEADS * DH].rearrange("p (h d) -> p h d", d=DH)
        m_part = sb("m_part", [P, 2, NB, 2])
        m_real = sb("m_real", [P, 2, NB])
        m_all = sb("m_all", [P, 2, NB])
        spread = sb("spread", [P, 2, NB, P], F32R)
        inv = sb("inv", [P, NCH, CH])
        den_t = sb("den_t", [P, NCH, CH])
        inv_16 = sb("inv_16", [P, NCH, CH // 32])
        heads_out = sb("heads_out", [P, PAIRS, N])
        wq_raw = heads_out[:, 0, 0:HEADS * DH]
        wout_sb = sb("wout_sb", [P, PAIRS, D])

        gate_raw = sb("gate_raw", [E, D])
        gate_t = sb("gate_t", [P, E])
        gate_hi = sb("gate_hi", [P, E], F32R)
        gate_lo = sb("gate_lo", [P, E], F32R)
        logits = sb("logits", [P, NT, E])
        top = sb("top", [P, NT, 8])
        rest = sb("rest", [P, NT, E])
        low = sb("low", [P, NT])
        comb = sb("comb", [P, NT, E])
        up_raw = kf_room[:, 0:4 * HID].rearrange("p (k m n) -> p k m n", k=2, m=2)
        up_hi = sb("up_hi", [P, 2, 2, HID], F32R)
        up_lo = sb("up_lo", [P, 2, 2, HID], F32R)
        down_w = sb("down_w", [P, 2, 3, D])
        gated = probs[:, 0, :, :]
        hidden = heads_out[:].rearrange("p a n -> p (a n)")[:, 0:6 * CH].rearrange("p (j i n) -> p j i n", j=2, i=3)

        scores = ctx.enter_context(nc.psum_tensor("scores", [P, 2, 2, CH], F32))
        o_ps = ctx.enter_context(nc.psum_tensor("o_ps", [P, NCH, CH], F32))
        misc = ctx.enter_context(nc.psum_tensor("misc", [P, 2, CH], F32))

        x_loaded = [sem(f"x_loaded{q}") for q in range(NT // 4)]
        c_loaded, w_loaded = sem("c_loaded"), sem("w_loaded")
        vec = sem("vec")
        var_ready, sqrt_done = sem("var_ready"), sem("sqrt_done")
        norm_done = sem("norm_done")
        turned = sem("turned")
        t_high, t_low = sem("t_high"), sem("t_low")
        consts_ready = sem("consts_ready")
        wsplit = sem("wsplit")
        kv_filled, kv_high, kv_copied, kv_low = sem("kv_filled"), sem("kv_high"), sem("kv_copied"), sem("kv_low")
        v_turned, v_copied = sem("v_turned"), sem("v_copied")
        null_filled, null_copied = sem("null_filled"), sem("null_copied")
        wcur_ready = sem("wcur_ready")
        q_filled, q_high, q_low, q_copied = sem("q_filled"), sem("q_high"), sem("q_low"), sem("q_copied")
        unit_filled, unit_max, real_max, head_max = (sem("unit_filled"), sem("unit_max"), sem("real_max"),
                                                     sem("head_max"))
        spread_ready, row_filled, row_copied = sem("spread_ready"), sem("row_filled"), sem("row_copied")
        scores_ready, probs_ready, av_done = sem("scores_ready"), sem("probs_ready"), sem("av_done")
        summed, sums_ready = sem("summed"), sem("sums_ready")
        den_filled, den_turned, inv_small, inv_wide = (sem("den_filled"), sem("den_turned"), sem("inv_small"),
                                                       sem("inv_wide"))
        inv_ready, o_done = sem("inv_ready"), sem("o_done")
        proj_filled, proj_copied = sem("proj_filled"), sem("proj_copied")
        stored = sem("stored")
        g_loaded, gate_turned, gate_split = sem("g_loaded"), sem("gate_turned"), sem("gate_split")
        logits_filled, logits_copied, exp_done = sem("logits_filled"), sem("logits_copied"), sem("exp_done")
        ew_loaded = [sem(f"ew_loaded{k}") for k in range(2)]
        ew_high, ew_split = sem("ew_high"), sem("ew_split")
        up_filled, silu_done, hidden_ready = sem("up_filled"), sem("silu_done"), sem("hidden_ready")
        down_filled, added = sem("down_filled"), sem("added")
        result_ready = sem("result_ready")
        block = ctx.enter_context(nc.Block())

        FILL = {(-1, 0): ["q"], (0, 0): ["q"], (1, 0): ["q"], (1, 2): ["q"],
                (2, 2): ["unit"], (3, 1): ["unit"], (3, 2): ["unit"],
                (4, 0): ["unit"], (4, 1): ["unit"], (4, 2): ["den"],
                (9, 0): ["unit"], (9, 1): ["unit"], (9, 2): ["unit"],
                (10, 0): ["unit"], (10, 1): ["unit"], (10, 2): ["row", "row"],
                (11, 1): ["unit"], (11, 2): ["unit"]}
        for t in range(5, 9):
            for place in range(3):
                FILL[t, place] = ["unit"]

        def fill_of(nxt):
            count, found = dict(q=0, unit=0, den=0, row=0), {}
            for place in sorted(FILL):
                found[place] = []
                for kind in FILL[place]:
                    if nxt or kind == "den":
                        found[place].append((kind, count[kind]))
                        count[kind] += 1
            assert not nxt or (count["unit"], count["q"], count["row"]) == (2 * U, 2 * NCH, NCH)
            return found

        STAGES = 4
        PREV_STAGE = {("q", i): i + 1 for i in range(STAGES)}
        THIS_STAGE = {("unit", 5 + i): i + 1 for i in range(STAGES)}

        def misc_uses(prev, nxt, proj):
            fill = fill_of(nxt)
            uses = [("den", -1, 1)] if prev else []
            uses += [("row", 0, i) for i in range(NCH, 2 * NCH)]
            for place in sorted(fill):
                if place == (1, 0) and proj:
                    uses += [("proj", 0, i) for i in range(NB)]
                uses += [(kind, 0 if kind == "den" else 1, i) for kind, i in fill[place]]
            return uses

        PER_PAIR = {"q": 2 * NCH, "row": 2 * NCH, "unit": 2 * U, "den": NCH}
        READ_BY = {"q": q_low, "row": row_copied, "unit": unit_max, "den": den_turned, "proj": proj_copied}

        def plan(g):
            return dict(prev=g > 0, nxt=g < B * PAIRS - 1, proj=g == PAIRS)

        def uses_of(g):
            if g < 0:
                return [("q", 1, i) for i in range(2 * NCH)] + [("unit", 1, i) for i in range(2 * U)] + \
                    [("row", 1, i) for i in range(NCH)]
            return misc_uses(**plan(g))

        def banks_of(g):
            start = 0
            for k in range(-1, g):
                start += len(uses_of(k))
            return {u: (start + n) % 2 for n, u in enumerate(uses_of(g))}

        def all_pairs(eng, body):
            for b in range(B):
                body(b * PAIRS, b * PAIRS, b)
                with eng.Fori(0, (PAIRS - 2) // 2) as i:
                    for k in (1, 2):
                        body(2 * i + (b * PAIRS + k), b * PAIRS + 2 + k, b)
                body((b + 1) * PAIRS - 1, (b + 1) * PAIRS - 1, b)

        NJ = TOK // CH
        pieces = [(0, P), (P, P), (2 * P, HID - 2 * P)]
        shared_pieces = [(0, P), (P, SHID - P)]
        E_LOADS = 16 * 4

        def pieces_of(s):
            return pieces if s else shared_pieces

        def units_before(number):
            return len(shared_pieces) * NJ + len(pieces) * NJ * (number - 1) if not isinstance(number, int) or number \
                else 0

        def all_experts(eng, body):
            for s in range(3):
                body(s, s)
            with eng.Fori(0, (E - 2) // 2) as i:
                for k in (3, 4):
                    body(2 * i + k, k)

        @block.sync
        def _(sp):
            for t0 in range(0, NT, 4):
                sp.dma_start(x_sb[:, t0:t0 + 4, :],
                             x.rearrange("b n d -> (b n) d").rearrange("(t p) d -> p t d", p=P)[:, t0:t0 + 4, :]
                             ).then_inc(x_loaded[t0 // 4], 16)
            for dst, src in ((ident, ident_f), (identb, ident_b), (maskt, mask_t), (maskn, mask_n), (maskf, mask_fix)):
                sp.dma_start(dst[:], src).then_inc(c_loaded, 16)
            sp.dma_start(wq_raw, wq).then_inc(w_loaded, 16)
            for j in range(2):
                sp.dma_start(wkv_raw[:, j, :], wkv).then_inc(w_loaded, 16)
                sp.dma_start(null_col[j * DH:(j + 1) * DH, :], null_kv.rearrange("(d a) -> d a", a=1)
                             ).then_inc(w_loaded, 16)
            for b in range(B):
                sp.dma_start(kf[:, b, 0:1], null_kv.rearrange("(d a) -> d a", a=1)).then_inc(w_loaded, 16)
            sp.dma_start(null_bc[:], null_kv.rearrange("(a d) -> a d", a=1).broadcast_to([P, DH])
                         ).then_inc(w_loaded, 16)
            sp.dma_start(wout_sb[:], wout.rearrange("(p k) n -> k p n", k=P)).then_inc(w_loaded, 16)
            sp.dma_start(gate_raw[:], gate_w).then_inc(g_loaded, 16)

            sp.wait_ge(v_turned, B + 1)
            sp.wait_ge(kv_low, B * NCH + B)

            def body(number, s):
                k = s % 2
                if s >= 2:
                    sp.wait_ge(down_filled, NJ * (number - 1))
                if s == 0:
                    srcs, hid = (sw1, sw3, sw2), SHID
                else:
                    e = number - 1
                    srcs = tuple(w[bass.ds(e, 1), :, :].rearrange("o a b -> (o a) b") for w in (w1, w3, w2))
                    hid = HID
                for j in range(2):
                    sp.dma_start(up_raw[:, k, j, 0:hid], srcs[j]).then_inc(ew_loaded[k], 16)
                whole = hid // P
                sp.dma_start(down_w[:, k, 0:whole, :],
                             srcs[2][0:whole * P, :].rearrange("(c p) d -> p c d", p=P)).then_inc(ew_loaded[k], 16)
                sp.dma_start(down_w[0:hid - whole * P, k, whole, :], srcs[2][whole * P:hid, :]
                             ).then_inc(ew_loaded[k], 16)

            all_experts(sp, body)
            for q in range(4):
                sp.wait_ge(result_ready, q + 1)
                sp.dma_start(out.rearrange("b n d -> (b n) d").rearrange("(t p) d -> p t d", p=P)[:, 4 * q:4 * q + 4, :],
                             xn[:, 4 * q:4 * q + 4, :]).then_inc(stored, 16)
            sp.wait_ge(stored, 16 * 4)

        W_LOADS = 16 * (1 + 4 + B + 2)

        @block.gpsimd
        def _(pool):
            pool.memset(ones[:], 1.0)
            pool.memset(m_part[:], LOWEST)
            pool.memset(row_sel[:, 0:DH].bitcast(F32), 0.0)
            pool.memset(row_sel[:, DH:DH + 1].bitcast(F32), 1.0).then_inc(consts_ready, 1)

            def body(number, g, b):
                for t in range(1, T):
                    if t not in summed_after:
                        continue
                    c, kb, first = tiles[t]
                    t0 = first_of[c]
                    slot = (t - 1) % NPB
                    if t == t0:
                        continue
                    pool.wait_ge(probs_ready, T * number + t + 1)
                    acc = psums[:, c, :, :]
                    if t == t0 + 1:
                        if g > 0:
                            pool.wait_ge(den_filled, NCH * (number - 1) + c + 1)
                        before = probs[:, (t0 - 1) % NPB, :, :]
                        pool.tensor_tensor(acc[:, :, first:CH], before[:, :, first:CH], probs[:, slot, :, first:CH],
                                           ALU.add).then_inc(summed, 1 if first else 2)
                        if first:
                            pool.tensor_scalar(acc[:, :, 0:first], before[:, :, 0:first], 1.0, None, ALU.mult
                                               ).then_inc(summed, 1)
                    else:
                        pool.wait_ge(summed, SUMS * number + summed_after[t] - 1)
                        pool.tensor_tensor(acc[:, :, first:CH], acc[:, :, first:CH], probs[:, slot, :, first:CH],
                                           ALU.add).then_inc(summed, 1)
                    if t == last_of[c] - NARROW:
                        pool.wait_ge(summed, SUMS * number + summed_after[t])
                        pool.tensor_tensor(acc[0:2, :, CH - 1], acc[0:2, :, CH - 1], probs_fix[:, g % 2, :, c],
                                           ALU.add).then_inc(sums_ready, 1)

            all_pairs(pool, body)

            def split_weights(number, s):
                k, hid = s % 2, HID if s else SHID
                pool.wait_ge(ew_loaded[k], (number - k) * (E_LOADS // 2) + E_LOADS)
                if s >= 2:
                    pool.wait_ge(up_filled, units_before(number - 1))
                pool.tensor_tensor(up_hi[:, k, :, 0:hid], up_raw[:, k, :, 0:hid],
                                   ones[:, 0:1].unsqueeze(2).broadcast_to([P, 2, hid]), ALU.mult).then_inc(ew_high, 1)
                pool.wait_ge(ew_high, number + 1)
                pool.tensor_tensor(up_lo[:, k, :, 0:hid], up_raw[:, k, :, 0:hid], up_hi[:, k, :, 0:hid].bitcast(F32),
                                   ALU.subtract).then_inc(ew_split, 1)

            all_experts(pool, split_weights)

        @block.scalar
        def _(act):
            act.wait_ge(var_ready, 1)
            act.activation(std[:], vare[:], ACT.Sqrt).then_inc(sqrt_done, 1)
            for j in range(NT // 4):
                act.wait_ge(turned, j + 1)
                act.activation(xt_hi[:, j * CH:(j + 1) * CH], scores[:, j // 2 % 2, j % 2, :], ACT.Copy
                               ).then_inc(t_high, 1)
            for j in range(B * NCH):
                b, c = divmod(j, NCH)
                act.wait_ge(kv_filled, j + 1)
                act.activation(k_hi[:, b, 1 + c * CH:1 + (c + 1) * CH], scores[:, j // 2 % 2, j % 2, :], ACT.Copy
                               ).then_inc(kv_high, 1)
            act.wait_ge(w_loaded, W_LOADS)
            for b in range(B):
                act.activation(k_hi[:, b, 0:1], null_col[:], ACT.Copy).then_inc(kv_high, 1)
            for b in range(B):
                act.wait_ge(v_turned, b + 1)
                act.activation(v_sb[:, b, :, :], o_ps[:, b, :].rearrange("p (k d) -> p k d", d=DH), ACT.Copy
                               ).then_inc(v_copied, 1)
            act.wait_ge(v_turned, B + 1)
            act.activation(v_fix[:], misc[0:2, 1, 0:B * DH].rearrange("p (b d) -> p b d", b=B), ACT.Copy
                           ).then_inc(v_copied, 1)
            act.wait_ge(null_filled, 1)
            act.activation(s_null[:], misc[:, 0, 0:NT * HEADS].rearrange("p (t h) -> p t h", h=HEADS), ACT.Copy
                           ).then_inc(null_copied, 1)

            def weights(pair):
                for dst, src in ((wcur_hi, wq_hi), (wcur_lo, wq_lo)):
                    for j in range(2):
                        act.activation(dst[:, :, j, :],
                                       src[:, bass.ds(pair * P, P)].bitcast(F32).rearrange("p (h d) -> p h d", h=2),
                                       ACT.Copy).then_inc(wcur_ready, 1)

            def high_part(number, g, i):
                par, bank = (g + 1) % 2, banks_of(g)["q", 1, i]
                h, c = divmod(i, NCH)
                act.wait_ge(q_filled, PER_PAIR["q"] * (number + 1) + i + 1)
                if i == 0 and g >= 1:
                    act.wait_ge(scores_ready, T * number)
                act.activation(q_split[0:DH, par, h, c * CH:(c + 1) * CH], misc[0:DH, bank, :], ACT.Copy
                               ).then_inc(q_copied, 1)
                act.activation(q_hi[:, par, h, c * CH:(c + 1) * CH], misc[:, bank, :], ACT.Copy).then_inc(q_high, 1)

            def copy_row(number, g, rel, i):
                h, c = divmod(i, NCH)
                act.wait_ge(row_filled, PER_PAIR["row"] * (number + rel) + i + 1)
                act.activation(q_hi[DH:DH + 1, (g + rel) % 2, h, c * CH:(c + 1) * CH],
                               misc[DH:DH + 1, banks_of(g)["row", rel, i], :], ACT.Copy).then_inc(row_copied, 1)

            def copy_rows(number, g, rel, h):
                for c in range(NCH):
                    copy_row(number, g, rel, h * NCH + c)

            act.wait_ge(wsplit, 4)
            weights(0)
            for i in range(2 * NCH):
                high_part(-1, -1, i)
            weights(1)
            copy_rows(-1, -1, 1, 0)

            def body(number, g, b):
                todo = plan(g)
                copy_rows(number, g, 0, 1)
                fill = fill_of(todo["nxt"])

                def filled(place):
                    for kind, i in fill.get(place, []):
                        if kind == "q":
                            high_part(number, g, i)
                            if i == 2 * NCH - 1 and g + 2 < B * PAIRS:
                                weights(number + 2 - b * PAIRS if g % PAIRS < PAIRS - 1 else 1)
                        if kind == "row":
                            copy_row(number, g, 1, i)

                filled((-1, 0))
                for t in range(T):
                    st = (g * T + t) % 2
                    if t:
                        filled((t - 1, 0))
                    act.wait_ge(scores_ready, T * number + t + 1)
                    if t == 0:
                        act.activation(probs_fix[:, g % 2, :, :], scores[0:2, st, :, 0:2], ACT.Exp
                                       ).then_inc(probs_ready, 1)
                        continue
                    c, kb, first = tiles[t]
                    slot = (t - 1) % NPB
                    if t > NPB or g > 0:
                        old, of = (t - NPB, number) if t > NPB else (TF + t - NPB, number - 1)
                        act.wait_ge(av_done, TF * of + old)
                        if old in summed_after:
                            act.wait_ge(summed, SUMS * of + summed_after[old])
                        else:
                            act.wait_ge(den_filled, NCH * of + tiles[old][0] + 1)
                    act.activation(probs[:, slot, :, first:CH], scores[:, st, :, first:CH], ACT.Exp
                                   ).then_inc(probs_ready, 1)
                    if t == 1 and todo["proj"]:
                        filled((0, 1))
                        filled((0, 2))
                        project_copies(0, banks_of(g))
                        continue
                    filled((t - 1, 1))
                    filled((t - 1, 2))
                filled((TF, 2))

            def project_copies(b, banks):
                for i in range(NB):
                    act.wait_ge(proj_filled, b * NB + i + 1)
                    bank = banks["proj", 0, i] if banks else i % 2
                    act.activation(attn[:, b * NB + i, :], misc[:, bank, 0:D], ACT.Copy).then_inc(proj_copied, 1)

            all_pairs(act, body)
            project_copies(B - 1, None)

            for n in (1, 2):
                act.wait_ge(var_ready, n + 1)
                act.activation(std[:], vare[:], ACT.Sqrt).then_inc(sqrt_done, 1)
            for j in range(NT // 4):
                act.wait_ge(turned, NT // 4 + j + 1)
                act.activation(xt_hi[:, j * CH:(j + 1) * CH], scores[:, j // 2 % 2, j % 2, :], ACT.Copy
                               ).then_inc(t_high, 1)
            act.wait_ge(logits_copied, 1)
            act.activation(rest[:], logits[:], ACT.Exp).then_inc(exp_done, 1)

            def silu(number, s):
                for j in range(NJ):
                    for i, (_, rows_) in enumerate(pieces_of(s)):
                        n = j * len(pieces_of(s)) + i
                        at = units_before(number) + n
                        act.wait_ge(up_filled, at + 1)
                        if s or n >= 2:
                            act.wait_ge(hidden_ready, at - 1)
                        act.activation(gated[0:rows_, n % 2, :], scores[0:rows_, n % 2, 0, :], ACT.Silu
                                       ).then_inc(silu_done, 1)

            all_experts(act, silu)
            act.wait_ge(var_ready, 4)
            act.activation(std[:], vare[:], ACT.Sqrt).then_inc(sqrt_done, 1)

        @block.tensor
        def _(pe):
            pe.wait_ge(c_loaded, 16 * 5)
            def turn_tokens(n):
                for t in range(NT):
                    j = t // 4
                    pe.wait_ge(norm_done, n * NT + t + 1)
                    mm = pe.transpose(scores[:, j // 2 % 2, j % 2, (t % 4) * P:(t % 4 + 1) * P], xn[:, t, :],
                                      ident[:])
                    if t % 4 == 3:
                        mm.then_inc(turned, 1)

            turn_tokens(0)
            pe.wait_ge(wsplit, 4)
            for j in range(B * NCH):
                pe.wait_ge(t_high, j + 1)
                pe.wait_ge(t_low, j + 1)
                dst = scores[:, j // 2 % 2, j % 2, :]
                sl = slice(j * CH, (j + 1) * CH)
                pe.matmul(dst, wkv_hi[:].rearrange("p a d -> p (a d)"), xt_hi[:, sl], start=True, stop=False)
                pe.matmul(dst, wkv_lo[:].rearrange("p a d -> p (a d)"), xt_hi[:, sl], start=False, stop=False)
                pe.matmul(dst, wkv_hi[:].rearrange("p a d -> p (a d)"), xt_lo[:, sl], start=False, stop=True
                          ).then_inc(kv_filled, 1)
            for t in range(NT):
                dst = misc[:, 0, t * HEADS:(t + 1) * HEADS]
                sl = slice(t * P, (t + 1) * P)
                pe.matmul(dst, xt_hi[:, sl], wn_hi[:], start=True, stop=False)
                pe.matmul(dst, xt_hi[:, sl], wn_lo[:], start=False, stop=False)
                mm = pe.matmul(dst, xt_lo[:, sl], wn_hi[:], start=False, stop=True)
            mm.then_inc(null_filled, 1)
            pe.wait_ge(kv_copied, B * NCH)
            for b in range(B):
                for kb in range(NB):
                    mm = pe.transpose(o_ps[:, b, kb * DH:(kb + 1) * DH], kf[:, b, kb * P:(kb + 1) * P],
                                      ident[0:DH, 0:DH])
                mm.then_inc(v_turned, 1)
            for b in range(B):
                mm = pe.transpose(misc[0:2, 1, b * DH:(b + 1) * DH], kf[:, b, CH:N + 1:CH], ident[0:DH, 0:DH])
            mm.then_inc(v_turned, 1)
            pe.wait_ge(null_copied, 1)
            pe.wait_ge(v_copied, B + 1)
            pe.wait_ge(kv_low, B * NCH + B)
            pe.wait_ge(kv_high, B * NCH + B)

            def take(g, number, kind, state):
                seq_before = uses_of(g - 1) if g >= 0 else []
                mine = uses_of(g)
                n = state[0]
                state[0] += 1
                assert mine[n][0] == kind, (mine[n], kind)
                seq = [(u, -1) for u in seq_before] + [(u, 0) for u in mine]
                at = len(seq_before) + n
                if at >= 2:
                    (k, rel, i), part = seq[at - 2]
                    if k == "proj":
                        pe.wait_ge(proj_copied, i + 1)
                    else:
                        pe.wait_ge(READ_BY[k], PER_PAIR[k] * (number + rel + part) + i + 1)
                return misc[:, banks_of(g)[mine[n]], :]

            def queries(g, number, i, state):
                nb = (g + 1) // PAIRS
                if i == 0:
                    pe.wait_ge(wcur_ready, 4 * (number + 2))
                h, c = divmod(i, NCH)
                dst = take(g, number, "q", state)
                sl = slice(nb * N + c * CH, nb * N + (c + 1) * CH)
                hi = wcur_hi[:, h, :, :].rearrange("p a d -> p (a d)")
                lo = wcur_lo[:, h, :, :].rearrange("p a d -> p (a d)")
                pe.matmul(dst, hi, xt_hi[:, sl], start=True, stop=False)
                pe.matmul(dst, hi, xt_lo[:, sl], start=False, stop=False)
                pe.matmul(dst, lo, xt_hi[:, sl], start=False, stop=True).then_inc(q_filled, 1)

            def maximum_unit(g, number, i, state):
                nb, par = (g + 1) // PAIRS, (g + 1) % 2
                h, u = divmod(i, U)
                qb, kc, n = units[u]
                if u == 0:
                    pe.wait_ge(q_low, PER_PAIR["q"] * (number + 1) + NCH * (h + 1))
                    pe.wait_ge(q_copied, PER_PAIR["q"] * (number + 1) + NCH * (h + 1))
                dst = take(g, number, "unit", state)
                diagonal = kc == qb // BPC
                mm = pe.matmul(dst[:, 0:n], q_split[:, par, h, qb * P:(qb + 1) * P],
                               k_hi[:, nb, 1 + kc * CH:1 + kc * CH + n], start=True, stop=True)
                if diagonal:
                    mm = pe.matmul(dst[:, n - P:n], identb[:], maskn[:], start=False, stop=True,
                               skip_group_check=True)
                mm.then_inc(unit_filled, 1)

            def row(g, number, rel, i, state):
                h, c = divmod(i, NCH)
                if c == 0:
                    pe.wait_ge(spread_ready, 2 * (number + rel) + h + 1)
                dst = take(g, number, "row", state)
                pe.matmul(dst[0:DH + 1, :], row_sel[:],
                          spread[:, h, c * BPC:(c + 1) * BPC, :].rearrange("p b q -> p (b q)"),
                          start=True, stop=True).then_inc(row_filled, 1)

            def score(g, number, t, b, h):
                st, par = (g * T + t) % 2, g % 2
                use = T * number + t
                if h == 0 and (t >= 2 or g > 0):
                    pe.wait_ge(probs_ready, use - 1)
                if t == 0:
                    qs, ks = slice(CH - 1, N, CH), slice(CH, N + 1, CH)
                    dst = scores[0:2, st, h, 0:2]
                else:
                    c, kb, first = tiles[t]
                    qs, ks = slice(c * CH + first, (c + 1) * CH), slice(kb * P, (kb + 1) * P)
                    dst = scores[:, st, h, first:CH]
                mm = pe.matmul(dst, k_hi[:, b, ks], q_split[:, par, h, qs], start=True, stop=False)
                if t == 0:
                    pe.wait_ge(row_copied, PER_PAIR["row"] * number + NCH * (h + 1))
                mm = pe.matmul(dst, k_lo[:, b, ks], q_hi[0:DH + 1, par, h, qs], start=False, stop=True)
                if t == 0:
                    mm = pe.matmul(dst, identb[0:2, 0:2], maskf[:], start=False, stop=True, skip_group_check=True)
                elif kb * P - 2 + P > c * CH:
                    skip = 0 if first else 2
                    m0 = P * kb - 2 + skip - CH * c
                    w = P + 2 - skip
                    mm = pe.matmul(scores[:, st, h, m0:m0 + w], identb[:], maskt[:, skip:skip + w],
                                   start=False, stop=True, skip_group_check=True)
                if h == 1:
                    mm.then_inc(scores_ready, 1)

            def weigh(g, number, t, b):
                c, kb, first = tiles[t]
                pe.wait_ge(probs_ready, T * number + t + 1)
                if t == first_of[c] and g > 0:
                    pe.wait_ge(o_done, NCH * (number - 1) + c + 1)
                slot = (t - 1) % NPB
                for h in range(2):
                    mm = pe.matmul(o_ps[h * DH:(h + 1) * DH, c, first:CH], v_sb[:, b, kb, :],
                                   probs[:, slot, h, first:CH], start=t == first_of[c], stop=t == last_of[c],
                                   skip_group_check=True)
                    if t == first_of[c]:
                        mm = pe.matmul(o_ps[h * DH:(h + 1) * DH, c, CH - 1:CH], v_fix[:, b, :],
                                       probs_fix[:, g % 2, h, c:c + 1], start=False, stop=False,
                                       skip_group_check=True)
                mm.then_inc(av_done, 1)

            def denominators(g, number, c, rel, state):
                pe.wait_ge(sums_ready, NCH * (number + rel) + c + 1)
                pe.wait_ge(probs_ready, T * (number + rel) + last_of[c] + 1)
                dst = take(g, number, "den", state) if state is not None else misc[:, 0, :]
                for h in range(2):
                    rows_ = slice(h * DH, (h + 1) * DH)
                    mm = pe.matmul(dst[rows_, :], ones[:], psums[:, c, h, :], start=True, stop=True,
                                   skip_group_check=True)
                    for t in range(last_of[c] - NARROW + 1, last_of[c] + 1):
                        first = tiles[t][2]
                        mm = pe.matmul(dst[rows_, first:CH], ones[:], probs[:, (t - 1) % NPB, h, first:CH],
                                       start=False, stop=True, skip_group_check=True)
                mm.then_inc(den_filled, 1)

            def project(b, g=None, number=None, state=None):
                pe.wait_ge(o_done, NCH * PAIRS * (b + 1))
                for i in range(NB):
                    if state is not None:
                        dst = take(g, number, "proj", state)
                    else:
                        dst = misc[:, i % 2, :]
                        if i < 2:
                            pe.wait_ge(den_turned, NCH * PAIRS * B)
                        else:
                            pe.wait_ge(proj_copied, b * NB + i - 1)
                    for p in range(PAIRS):
                        mm = pe.matmul(dst[:, 0:D], heads_out[:, p, i * P:(i + 1) * P], wout_sb[:, p, :],
                                       start=p == 0, stop=p == PAIRS - 1)
                    mm.then_inc(proj_filled, 1)

            state = [0]
            for i in range(2 * NCH):
                queries(-1, -1, i, state)
            pe.wait_ge(consts_ready, 1)
            for i in range(2 * U):
                maximum_unit(-1, -1, i, state)
            for i in range(NCH):
                row(-1, -1, 1, i, state)

            def body(number, g, b):
                todo = plan(g)
                state = [0]
                fill = fill_of(todo["nxt"])

                def make(place):
                    for kind, i in fill.get(place, []):
                        if kind == "q":
                            queries(g, number, i, state)
                        elif kind == "unit":
                            maximum_unit(g, number, i, state)
                        elif kind == "den":
                            denominators(g, number, 0, 0, state)
                        else:
                            row(g, number, 1, i, state)

                if todo["prev"]:
                    denominators(g, number, 1, -1, state)
                for i in range(NCH, 2 * NCH):
                    row(g, number, 0, i, state)
                make((-1, 0))
                for h in range(2):
                    score(g, number, 0, b, h)
                for t in range(T):
                    if t + 1 < T:
                        score(g, number, t + 1, b, 0)
                    if t == 1 and todo["proj"]:
                        project(0, g, number, state)
                    make((t, 0))
                    if t + 1 < T:
                        score(g, number, t + 1, b, 1)
                    make((t, 1))
                    if t:
                        weigh(g, number, t, b)
                    make((t, 2))
                if not todo["nxt"]:
                    pe.wait_ge(den_turned, NCH * number + 1)
                    denominators(g, number, 1, 0, None)

            all_pairs(pe, body)
            project(B - 1)

            pe.wait_ge(g_loaded, 16)
            pe.wait_ge(proj_copied, NT)
            pe.transpose(misc[:, 0, 0:E], gate_raw[:], ident[0:E, 0:E]).then_inc(gate_turned, 1)
            pe.wait_ge(probs_ready, T * B * PAIRS)
            turn_tokens(1)
            pe.wait_ge(gate_split, 2)
            for t in range(NT):
                pe.wait_ge(t_low, NT // 4 + t // 4 + 1)
                sl = slice(t * P, (t + 1) * P)
                dst = misc[:, 1, t * E:(t + 1) * E]
                pe.matmul(dst, xt_hi[:, sl], gate_hi[:], start=True, stop=False)
                pe.matmul(dst, xt_hi[:, sl], gate_lo[:], start=False, stop=False)
                mm = pe.matmul(dst, xt_lo[:, sl], gate_hi[:], start=False, stop=True)
            mm.then_inc(logits_filled, 1)

            def up(number, s, j):
                k, sl = s % 2, slice(j * CH, (j + 1) * CH)
                for i, (r0, rows_) in enumerate(pieces_of(s)):
                    n = j * len(pieces_of(s)) + i
                    at = units_before(number) + n
                    if s or n >= 2:
                        pe.wait_ge(hidden_ready, at - 1)
                    for m in range(2):
                        dst = scores[0:rows_, n % 2, m, :]
                        hi, lo = up_hi[:, k, m, r0:r0 + rows_], up_lo[:, k, m, r0:r0 + rows_]
                        pe.matmul(dst, hi, xt_hi[:, sl], start=True, stop=False)
                        pe.matmul(dst, hi, xt_lo[:, sl], start=False, stop=False)
                        mm = pe.matmul(dst, lo, xt_hi[:, sl], start=False, stop=True)
                    mm.then_inc(up_filled, 1)

            def down(number, s, j):
                k, ps = s % 2, pieces_of(s)
                pe.wait_ge(hidden_ready, units_before(number) + (j + 1) * len(ps))
                if s or j >= 2:
                    pe.wait_ge(added, NJ * number + j - 1)
                for t in range(BPC):
                    for i, (_, rows_) in enumerate(ps):
                        mm = pe.matmul(o_ps[:, j % 2, t * P:(t + 1) * P], hidden[0:rows_, j % 2, i, t * P:(t + 1) * P],
                                       down_w[0:rows_, k, i, :], start=i == 0, stop=i == len(ps) - 1)
                mm.then_inc(down_filled, 1)

            def experts(number, s):
                pe.wait_ge(ew_split, number + 1)
                for j in range(NJ):
                    up(number, s, j)
                    if j:
                        down(number, s, j - 1)
                    elif s:
                        down(number - 1, 0 if s == 1 else s - 1, NJ - 1)

            all_experts(pe, experts)
            down(E, E, NJ - 1)

        @block.vector
        def _(dve):
            steps = [0]

            def link(ins):
                steps[0] += 1
                ins.then_inc(vec, 1)
                dve.wait_ge(vec, steps[0])

            def moments(n, src):
                for t in range(NT):
                    if n == 0 and t % 4 == 0:
                        dve.wait_ge(x_loaded[t // 4], 16)
                    if n == 1:
                        dve.wait_ge(proj_copied, t + 1)
                    done = dve.bn_stats(stats[:, t, :], src[:, t, :])
                link(done)
                for t in range(NT):
                    done = dve.bn_aggr(mv[:, t, :], stats[:, t, :])
                link(done)
                dve.tensor_scalar(vare[:], mv[:, :, 1], EPS, None, ALU.add).then_inc(var_ready, 1)
                dve.wait_ge(sqrt_done, n + 1)
                link(dve.reciprocal(rstd[:], std[:]))

            def normalize_tokens(src):
                for t in range(NT):
                    dve.tensor_scalar(xn[:, t, :], src[:, t, :], mv[:, t, 0:1], rstd[:, t:t + 1], ALU.subtract,
                                      ALU.mult).then_inc(norm_done, 1)

            def low_tokens(n):
                for j in range(NT // 4):
                    dve.wait_ge(t_high, n * (NT // 4) + j + 1)
                    dve.tensor_tensor(xt_lo[:, j * CH:(j + 1) * CH], scores[:, j // 2 % 2, j % 2, :],
                                      xt_hi[:, j * CH:(j + 1) * CH].bitcast(F32), ALU.subtract).then_inc(t_low, 1)

            moments(0, x_sb)
            normalize_tokens(x_sb)
            dve.wait_ge(w_loaded, W_LOADS)
            dve.wait_ge(c_loaded, 16 * 5)
            link(dve.tensor_scalar(wq_raw, wq_raw, SCALE, None, ALU.mult))
            WQ = HEADS * DH
            dve.tensor_copy(wq_hi[:, 0:WQ], wq_raw).then_inc(wsplit, 1)
            dve.tensor_copy(wkv_hi[:], wkv_raw[:]).then_inc(wsplit, 1)
            dve.wait_ge(wsplit, 2)
            dve.tensor_copy(wq_hi[:, WQ:WQ + P], wq_hi[:, 0:P].bitcast(F32))
            link(dve.tensor_tensor(wq_lo[:, 0:WQ], wq_raw, wq_hi[:, 0:WQ].bitcast(F32), ALU.subtract))
            dve.tensor_copy(wq_lo[:, WQ:WQ + P], wq_lo[:, 0:P].bitcast(F32)).then_inc(wsplit, 1)
            dve.tensor_tensor(wkv_lo[:], wkv_raw[:], wkv_hi[:].bitcast(F32), ALU.subtract)
            link(dve.tensor_tensor(wn_prod, wq_raw.rearrange("p (h d) -> p h d", d=DH),
                                   null_bc[:].unsqueeze(1).broadcast_to([P, HEADS, DH]), ALU.mult))
            link(dve.tensor_reduce(wn[:], wn_prod, AX_X, ALU.add))
            link(dve.tensor_copy(wn_hi[:], wn[:]))
            dve.tensor_scalar(neg_ident[:], ident[:], -1.0, None, ALU.mult)
            dve.tensor_tensor(wn_lo[:], wn[:], wn_hi[:].bitcast(F32), ALU.subtract).then_inc(wsplit, 1)
            low_tokens(0)
            for j in range(B * NCH):
                b, c = divmod(j, NCH)
                sl = slice(1 + c * CH, 1 + (c + 1) * CH)
                dve.wait_ge(kv_high, j + 1)
                dve.tensor_copy(kf[:, b, sl], scores[0:DH, j // 2 % 2, j % 2, :]).then_inc(kv_copied, 1)
                dve.tensor_tensor(k_lo[0:DH, b, sl], scores[0:DH, j // 2 % 2, j % 2, :],
                                  k_hi[0:DH, b, sl].bitcast(F32), ALU.subtract).then_inc(kv_low, 1)
            dve.memset(k_lo[DH:DH + 1, :, :].bitcast(F32), 1.0)
            dve.wait_ge(kv_high, B * NCH + B)
            for b in range(B):
                dve.tensor_tensor(k_lo[0:DH, b, 0:1], kf[:, b, 0:1], k_hi[0:DH, b, 0:1].bitcast(F32), ALU.subtract
                                  ).then_inc(kv_low, 1)

            def low_part(g, number, i):
                par, bank = (g + 1) % 2, banks_of(g)["q", 1, i]
                h, c = divmod(i, NCH)
                sl = slice(c * CH, (c + 1) * CH)
                dve.wait_ge(q_high, PER_PAIR["q"] * (number + 1) + i + 1)
                dve.tensor_tensor(q_split[DH:P, par, h, sl], misc[DH:P, bank, :],
                                  q_hi[DH:P, par, h, sl].bitcast(F32), ALU.subtract).then_inc(q_low, 1)

            def unit(g, number, i):
                h, u = divmod(i, U)
                qb, kc, n = units[u]
                bank = banks_of(g)["unit", 1, i]
                dve.wait_ge(unit_filled, PER_PAIR["unit"] * (number + 1) + i + 1)
                dve.tensor_reduce(m_part[:, h, qb, kc:kc + 1], misc[:, bank, 0:n], AX_X, ALU.max
                                  ).then_inc(unit_max, 1)
                if u == U - 1:
                    whole_max(g, number, h)

            def whole_max(g, number, h):
                nb = (g + 1) // PAIRS
                head = 2 * (number + 1 - nb * PAIRS) + h
                dve.wait_ge(unit_max, PER_PAIR["unit"] * (number + 1) + (h + 1) * U)
                dve.tensor_reduce(m_real[:, h, :], m_part[:, h, :, :], AX_X, ALU.max).then_inc(real_max, 1)
                dve.wait_ge(real_max, 2 * (number + 1) + h + 1)
                dve.tensor_tensor(m_all[:, h, :], m_real[:, h, :],
                                  s_null[:, nb * NB:(nb + 1) * NB, bass.ds(head, 1)].rearrange("p t o -> p (t o)"),
                                  ALU.max).then_inc(head_max, 1)
                dve.wait_ge(head_max, 2 * (number + 1) + h + 1)
                if g >= 0:
                    dve.wait_ge(row_filled, PER_PAIR["row"] * number + NCH * (h + 1))
                dve.tensor_tensor(spread[:, h, :, :], neg_ident[:].unsqueeze(1).broadcast_to([P, NB, P]),
                                  m_all[:, h, :].unsqueeze(2).broadcast_to([P, NB, P]), ALU.mult
                                  ).then_inc(spread_ready, 1)

            def normalize(g, number, c, rel, stage, bank=None):
                pair = number + rel - ((g + rel) // PAIRS) * PAIRS
                done = NCH * (number + rel) + c + 1
                if stage == 0:
                    dve.wait_ge(den_filled, done)
                    dve.transpose(den_t[:, c, :], misc[:, bank, :]).then_inc(den_turned, 1)
                elif stage == 1:
                    dve.wait_ge(den_turned, done)
                    dve.reciprocal(inv_16[:, c, :], den_t[:, c, 0:CH:32]).then_inc(inv_small, 1)
                elif stage == 2:
                    dve.wait_ge(inv_small, done)
                    dve.tensor_copy(den_t[:, c, :].rearrange("p (j k) -> p j k", k=32),
                                    inv_16[:, c, :].unsqueeze(2).broadcast_to([P, CH // 32, 32])
                                    ).then_inc(inv_wide, 1)
                elif stage == 3:
                    dve.wait_ge(inv_wide, done)
                    dve.transpose(inv[:, c, :], den_t[:, c, :]).then_inc(inv_ready, 1)
                else:
                    dve.wait_ge(inv_ready, done)
                    dve.wait_ge(av_done, TF * (number + rel) + last_of[c])
                    if g == PAIRS and rel == 0:
                        dve.wait_ge(proj_filled, NB)
                    dve.tensor_tensor(
                        heads_out[:, bass.ds(pair, 1), c * CH:(c + 1) * CH].rearrange("p o n -> p (o n)"),
                        o_ps[:, c, :], inv[:, c, :], ALU.mult).then_inc(o_done, 1)

            dve.wait_ge(null_copied, 1)
            dve.wait_ge(consts_ready, 1)
            for i in range(2 * NCH):
                low_part(-1, -1, i)
            for i in range(2 * U):
                unit(-1, -1, i)

            def body(number, g, b):
                todo = plan(g)
                for kind, rel, i in uses_of(g):
                    if kind == "den":
                        normalize(g, number, i, rel, 0, banks_of(g)[kind, rel, i])
                    elif kind == "q":
                        low_part(g, number, i)
                    elif kind == "unit":
                        unit(g, number, i)
                    if todo["prev"] and not todo["proj"] and (kind, i) in PREV_STAGE:
                        normalize(g, number, 1, -1, PREV_STAGE[kind, i])
                    if (kind, i) in THIS_STAGE:
                        normalize(g, number, 0, 0, THIS_STAGE[kind, i])
                    if kind == "den" and (not todo["nxt"] or todo["proj"] and i == 1):
                        for stage in range(1, STAGES + 1):
                            normalize(g, number, i, rel, stage)
                if not todo["nxt"]:
                    for stage in range(STAGES + 1):
                        normalize(g, number, 1, 0, stage, 0)

            all_pairs(dve, body)

            moments(1, attn)
            for t in range(NT):
                done = dve.tensor_scalar(xn[:, t, :], attn[:, t, :], mv[:, t, 0:1], rstd[:, t:t + 1], ALU.subtract,
                                         ALU.mult)
            link(done)
            link(dve.tensor_tensor(x_sb[:], x_sb[:], xn[:], ALU.add))
            moments(2, x_sb)
            normalize_tokens(x_sb)
            dve.wait_ge(gate_turned, 1)
            link(dve.tensor_copy(gate_t[:], misc[:, 0, 0:E]))
            dve.tensor_copy(gate_hi[:], gate_t[:]).then_inc(gate_split, 1)
            dve.wait_ge(gate_split, 1)
            dve.tensor_tensor(gate_lo[:], gate_t[:], gate_hi[:].bitcast(F32), ALU.subtract).then_inc(gate_split, 1)
            low_tokens(1)
            dve.wait_ge(logits_filled, 1)
            ps = misc[:, 1, 0:NT * E].rearrange("p (t e) -> p t e", e=E)
            link(dve.tensor_reduce(low[:], ps, AX_X, ALU.max))
            dve.tensor_tensor(logits[:], ps, low[:].unsqueeze(2).broadcast_to([P, NT, E]), ALU.subtract
                              ).then_inc(logits_copied, 1)
            dve.wait_ge(exp_done, 1)
            link(dve.tensor_reduce(low[:], rest[:], AX_X, ALU.add))
            link(dve.reciprocal(low[:], low[:]))
            link(dve.tensor_tensor(comb[:], rest[:], low[:].unsqueeze(2).broadcast_to([P, NT, E]), ALU.mult))
            for t in range(NT):
                done = dve.max(top[:, t, :], comb[:, t, :])
            link(done)
            link(dve.memset(top[:, :, 2:8], -1.0))
            for t in range(NT):
                done = dve.match_replace(rest[:, t, :], top[:, t, :], comb[:, t, :], 0.0)
            link(done)
            link(dve.tensor_tensor(comb[:], comb[:], rest[:], ALU.subtract))

            def products(number, s, j):
                for i, (_, rows_) in enumerate(pieces_of(s)):
                    n = j * len(pieces_of(s)) + i
                    at = units_before(number) + n
                    dve.wait_ge(silu_done, at + 1)
                    if i == 0 and (s or j >= 2):
                        dve.wait_ge(down_filled, NJ * number + j - 1)
                    dve.tensor_tensor(hidden[0:rows_, j % 2, i, :], gated[0:rows_, n % 2, :],
                                      scores[0:rows_, n % 2, 1, :], ALU.mult).then_inc(hidden_ready, 1)

            def add(number, s, j):
                dve.wait_ge(down_filled, NJ * number + j + 1)
                if s == 0:
                    dve.tensor_copy(attn[:, j * BPC:(j + 1) * BPC, :],
                                    o_ps[:, j % 2, :].rearrange("p (t d) -> p t d", d=D)).then_inc(added, 1)
                    return
                dve.wait_ge(added, NJ * (number - 1) + j + 1)
                for t in range(BPC):
                    tt = j * BPC + t
                    done = dve.scalar_tensor_tensor(out=attn[:, tt, :], in0=o_ps[:, j % 2, t * P:(t + 1) * P],
                                                    scalar=comb[:, tt, bass.ds(number - 1, 1)], in1=attn[:, tt, :],
                                                    op0=ALU.mult, op1=ALU.add)
                done.then_inc(added, 1)

            def experts(number, s):
                for j in range(NJ):
                    products(number, s, j)
                    if j:
                        add(number, s, j - 1)
                    elif s:
                        add(number - 1, s - 1, NJ - 1)

            all_experts(dve, experts)
            add(E, E, NJ - 1)

            dve.wait_ge(added, NJ * (E + 1))
            moments(3, attn)
            for t in range(NT):
                done = dve.tensor_scalar(attn[:, t, :], attn[:, t, :], mv[:, t, 0:1], rstd[:, t:t + 1], ALU.subtract,
                                         ALU.mult)
            link(done)
            for q in range(4):
                sl = slice(4 * q, 4 * q + 4)
                dve.tensor_tensor(xn[:, sl, :], x_sb[:, sl, :], attn[:, sl, :], ALU.add).then_inc(result_ready, 1)


_INS = ["L0_attn_x", "L0_attn_Wq", "L0_attn_Wkv", "L0_attn_null_kv", "L0_attn_Wout", "L0_ffn_gate_w", "L0_ffn_w1",
        "L0_ffn_w2", "L0_ffn_w3", "L0_ffn_sw1", "L0_ffn_sw2", "L0_ffn_sw3"]


def kernel(**inputs):
    import ml_dtypes
    import concourse.bacc as bacc
    from concourse.bass_utils import run_bass_kernel_spmd

    nc = bacc.Bacc("TRN2", target_bir_lowering=False, num_devices=1)
    arrays, args = {}, []

    def give(name, a):
        arrays[name] = a
        args.append(nc.dram_tensor(name, a.shape, mybir.dt.from_np(a.dtype), kind="ExternalInput").ap())

    for name in _INS:
        give(f"in_{name}_dram", np.ascontiguousarray(inputs[name]))
    bf16 = ml_dtypes.bfloat16
    give("ident_f", np.eye(P, dtype=np.float32))
    give("ident_b", np.eye(P, dtype=np.float32).astype(bf16))
    key, query = np.arange(P)[:, None], np.arange(-2, P)[None, :]
    give("mask_t", np.where(key > query + 1, MASKED, 0).astype(bf16))
    give("mask_n", np.where(np.arange(P)[None, :] > np.arange(P)[:, None], MASKED, 0).astype(bf16))
    give("mask_fix", np.where(np.eye(2) == 0, MASKED, 0).astype(bf16))
    shape = inputs["L0_attn_x"].shape
    args.append(nc.dram_tensor("out_0_dram", shape, F32, kind="ExternalOutput").ap())
    sandwich_layer(nc, *args)
    r = run_bass_kernel_spmd(nc, [arrays], core_ids=[0])
    return r.results[0]["out_0_dram"]
```

```python
from contextlib import ExitStack

import numpy as np

import concourse.bass as bass
from concourse import mybir

F32 = mybir.dt.float32
F32R = mybir.dt.float32r
BF16 = mybir.dt.bfloat16
ALU = mybir.AluOpType
ACT = mybir.ActivationFunctionType
AX_X = mybir.AxisListType.X

P = 128
CH = 512
EPS = 1e-5
MASKED = -1.0e38
LOWEST = -3.0e38


def sandwich_layer(nc, x, wq, wkv, null_kv, wout, gate_w, w1, w2, w3, sw1, sw2, sw3, ident_f, ident_b,
                   mask_t, mask_n, mask_fix, out):
    B, N, D = x.shape
    DH = null_kv.shape[0]
    HEADS = wq.shape[1] // DH
    PAIRS = HEADS // 2
    TOK = B * N
    NT = TOK // P
    NB = N // P
    NCH = N // CH
    BPC = CH // P
    NJ = TOK // CH
    E, _, HID = w1.shape
    SHID = sw1.shape[1]
    SCALE = float(DH) ** -0.5
    assert D == P and DH == 64 and N == 1024 and NCH == 2
    assert HID > 2 * P and HID <= 3 * P and SHID > P and SHID <= 2 * P

    tiles = [None]
    for c in range(NCH):
        for kb in range(BPC * (c + 1)):
            first = P * kb - 2 - CH * c if P * kb - 1 > CH * c else 0
            tiles.append((c, kb, first))
    T = len(tiles)
    TF = T - 1
    last_of = [max(t for t in range(1, T) if tiles[t][0] == c) for c in range(NCH)]
    first_of = [min(t for t in range(1, T) if tiles[t][0] == c) for c in range(NCH)]

    units = [(qb, kc, min(P * (qb + 1) - CH * kc, CH)) for qb in reversed(range(NB)) for kc in range(qb // BPC + 1)]
    U = len(units)
    NPB = 3
    NARROW = 0
    summed_after, SUMS = {}, 0
    for c in range(NCH):
        for t in range(first_of[c], last_of[c] - NARROW + 1):
            SUMS += 1
            summed_after[t] = SUMS
        summed_after[first_of[c]] += 1

    with ExitStack() as ctx:
        def sb(name, shape, dt=F32):
            return ctx.enter_context(nc.sbuf_tensor(name, shape, dt))

        def sem(name):
            return ctx.enter_context(nc.semaphore(name))

        x_sb = sb("x_sb", [P, NT, D])
        xn = sb("xn", [P, NT, D])
        xt_hi = sb("xt_hi", [P, TOK], F32R)
        xt_lo = sb("xt_lo", [P, TOK], F32R)
        stats = sb("stats", [P, NT, 6])
        mv = sb("mv", [P, NT, 2])
        vare = sb("vare", [P, NT])
        std = sb("std", [P, NT])
        rstd = sb("rstd", [P, NT])
        attn = sb("attn", [P, NT, D])
        ident = sb("ident", [P, P])
        neg_ident = sb("neg_ident", [P, P])
        identb = sb("identb", [P, P], BF16)
        maskt = sb("maskt", [P, P + 2], BF16)
        maskn = sb("maskn", [P, P], BF16)
        maskf = sb("maskf", [2, 2], BF16)
        ones = sb("ones", [P, DH])
        row_sel = sb("row_sel", [P, DH + 1], F32R)
        wq_hi = sb("wq_hi", [P, HEADS * DH + P], F32R)
        wq_lo = sb("wq_lo", [P, HEADS * DH + P], F32R)
        wcur_hi = sb("wcur_hi", [P, 2, 2, DH], F32R)
        wcur_lo = sb("wcur_lo", [P, 2, 2, DH], F32R)
        wkv_raw = sb("wkv_raw", [P, 2, DH])
        wkv_hi = sb("wkv_hi", [P, 2, DH], F32R)
        wkv_lo = sb("wkv_lo", [P, 2, DH], F32R)
        null_bc = sb("null_bc", [P, DH])
        null_col = sb("null_col", [P, 1])
        wn = sb("wn", [P, HEADS])
        wn_hi = sb("wn_hi", [P, HEADS], F32R)
        wn_lo = sb("wn_lo", [P, HEADS], F32R)
        s_null = sb("s_null", [P, NT, HEADS])
        kf_room = sb("kf_room", [P, B * (N + 2)])
        kf = kf_room[0:DH, :].rearrange("p (b n) -> p b n", b=B)
        k_hi = sb("k_hi", [P, B, N + 2], F32R)
        k_lo = sb("k_lo", [DH + 1, B, N + 2], F32R)
        v_sb = sb("v_sb", [P, B, NB, DH])
        v_fix = sb("v_fix", [2, B, DH])
        q_split = sb("q_split", [P, 2, 2, N], F32R)
        q_hi = sb("q_hi", [P, 2, 2, N], F32R)
        probs = sb("probs", [P, NPB, 2, CH])
        probs_fix = sb("probs_fix", [2, 2, 2, 2])
        psums = sb("psums", [P, NCH, 2, CH])
        psums_flat = psums[:].rearrange("p c h n -> p (c h n)")
        wn_prod = psums_flat[:, 0:HEADS * DH].rearrange("p (h d) -> p h d", d=DH)
        wq_scaled = psums_flat[:, HEADS * DH:2 * HEADS * DH]
        m_part = sb("m_part", [P, 2, NB, 2])
        m_real = sb("m_real", [P, 2, NB])
        m_all = sb("m_all", [P, 2, NB])
        spread = sb("spread", [P, 2, NB, P], F32R)
        inv = sb("inv", [P, NCH, CH])
        den_t = sb("den_t", [P, NCH, CH])
        inv_16 = sb("inv_16", [P, NCH, CH // 32])
        heads_out = sb("heads_out", [P, PAIRS, N])
        wq_raw = heads_out[:, 0, 0:HEADS * DH]
        wout_sb = sb("wout_sb", [P, PAIRS, D])

        gate_raw = sb("gate_raw", [E, D])
        gate_t = sb("gate_t", [P, E])
        gate_hi = sb("gate_hi", [P, E], F32R)
        gate_lo = sb("gate_lo", [P, E], F32R)
        logits = sb("logits", [P, NT, E])
        top = sb("top", [P, NT, 8])
        rest = sb("rest", [P, NT, E])
        low = sb("low", [P, NT])
        comb = sb("comb", [P, NT, E])
        up_raw = kf_room[:, 0:4 * HID].rearrange("p (k m n) -> p k m n", k=2, m=2)
        up_hi = sb("up_hi", [P, 2, 2, HID], F32R)
        up_lo = sb("up_lo", [P, 2, 2, HID], F32R)
        down_w = sb("down_w", [P, 2, 3, D])
        gated = probs[:, 0, :, :]
        hidden = heads_out[:].rearrange("p a n -> p (a n)")[:, 0:6 * CH].rearrange("p (j i n) -> p j i n", j=2, i=3)

        scores = ctx.enter_context(nc.psum_tensor("scores", [P, 2, 2, CH], F32))
        o_ps = ctx.enter_context(nc.psum_tensor("o_ps", [P, NCH, CH], F32))
        misc = ctx.enter_context(nc.psum_tensor("misc", [P, 2, CH], F32))

        x_loaded = [sem(f"x_loaded{q}") for q in range(NT // 4)]
        ident_loaded, w_loaded, null_loaded = sem("ident_loaded"), sem("w_loaded"), sem("null_loaded")
        c_loaded, wout_loaded = sem("c_loaded"), sem("wout_loaded")
        vec = sem("vec")
        var_ready, sqrt_done = sem("var_ready"), sem("sqrt_done")
        norm_done = sem("norm_done")
        turned = sem("turned")
        t_high, t_low = sem("t_high"), sem("t_low")
        consts_ready = sem("consts_ready")
        w_scaled, w_high, w_low = sem("w_scaled"), sem("w_high"), sem("w_low")
        wkv_high, wkv_low, wn_multiplied, wn_split = (sem("wkv_high"), sem("wkv_low"), sem("wn_multiplied"),
                                                      sem("wn_split"))
        kv_filled, kv_high, kv_copied, kv_low = sem("kv_filled"), sem("kv_high"), sem("kv_copied"), sem("kv_low")
        v_turned, v_copied = sem("v_turned"), sem("v_copied")
        null_filled, null_copied = sem("null_filled"), sem("null_copied")
        wcur_ready = sem("wcur_ready")
        q_filled, q_high, q_low, q_copied = sem("q_filled"), sem("q_high"), sem("q_low"), sem("q_copied")
        unit_filled, unit_max, real_max, head_max = (sem("unit_filled"), sem("unit_max"), sem("real_max"),
                                                     sem("head_max"))
        spread_ready, row_filled, row_copied = sem("spread_ready"), sem("row_filled"), sem("row_copied")
        scores_ready, probs_ready, av_done = sem("scores_ready"), sem("probs_ready"), sem("av_done")
        summed, sums_ready = sem("summed"), sem("sums_ready")
        den_filled, den_turned, inv_small, inv_wide = (sem("den_filled"), sem("den_turned"), sem("inv_small"),
                                                       sem("inv_wide"))
        inv_ready, o_done = sem("inv_ready"), sem("o_done")
        proj_filled, proj_copied = sem("proj_filled"), sem("proj_copied")
        rest_filled, rest_added = sem("rest_filled"), sem("rest_added")
        stored = sem("stored")
        g_loaded, gate_turned, gate_split = sem("g_loaded"), sem("gate_turned"), sem("gate_split")
        logits_filled, logits_copied, exp_done = sem("logits_filled"), sem("logits_copied"), sem("exp_done")
        ew_loaded = [sem(f"ew_loaded{k}") for k in range(2)]
        ew_high, ew_split = sem("ew_high"), sem("ew_split")
        up_filled, silu_done, hidden_ready = sem("up_filled"), sem("silu_done"), sem("hidden_ready")
        down_filled, added = sem("down_filled"), sem("added")
        result_ready = sem("result_ready")
        block = ctx.enter_context(nc.Block())

        FILL = {(-1, 0): ["past", "row_b", "row_b", "q"], (0, 1): ["q"], (1, 1): ["q"], (1, 2): ["q"],
                (3, 1): ["unit", "unit"], (3, 2): ["unit"], (4, 0): ["unit"], (4, 1): ["unit"],
                (4, 2): ["proj", "unit"], (5, 1): ["unit", "den"], (5, 2): ["unit", "unit"], (6, 0): ["unit"],
                (6, 1): ["unit"], (7, 0): ["unit", "unit"], (7, 1): ["unit"], (7, 2): ["unit"], (8, 0): ["unit"],
                (8, 2): ["unit"], (9, 1): ["unit", "unit"], (9, 2): ["unit", "unit"], (10, 1): ["unit"],
                (10, 2): ["row_a"], (11, 0): ["row_a"], (11, 2): ["unit", "unit"]}
        FILL_LAST = [(3 + i, 1) for i in range(NB)]
        REST_PLACE = (NB + 3, 1)
        TIMES = {"q": 2 * NCH, "unit": 2 * U, "row_a": NCH, "row_b": NCH, "den": 1, "past": 1, "proj": 1}
        assert all(sum(f.count(kind) for f in FILL.values()) == n for kind, n in TIMES.items())

        def plan(g):
            kinds = ["row_b", "den"]
            if g > 0:
                kinds.append("past")
            if g < B * PAIRS - 1:
                kinds += ["q", "unit", "row_a"]
            if g == PAIRS:
                kinds.append("proj")
            return kinds

        def fill_of(g):
            count, found = dict.fromkeys(TIMES, 0), {}
            for place in sorted(set(FILL) | set(FILL_LAST) | {REST_PLACE}):
                found[place] = []
                if g == B * PAIRS - 1 and place in FILL_LAST:
                    found[place].append(("part", 0, FILL_LAST.index(place)))
                if g == B * PAIRS - 1 and place == REST_PLACE:
                    found[place].append(("rest", 0, 0))
                for kind in FILL.get(place, []):
                    if kind not in plan(g):
                        continue
                    n = count[kind]
                    count[kind] += 1
                    found[place].append({"q": ("q", 1, n), "unit": ("unit", 1, n), "row_a": ("row", 1, n),
                                         "row_b": ("row", 0, NCH + n), "den": ("den", 0, 0),
                                         "past": ("den", -1, 1), "proj": ("proj", 0, 0)}[kind])
            return found

        PER_PAIR = {"q": 2 * NCH, "row": 2 * NCH, "unit": 2 * U, "den": NCH, "rest": 0}
        READ_BY = {"q": q_low, "row": row_copied, "unit": unit_max, "den": den_turned, "rest": rest_added}

        def uses_of(g):
            if g < 0:
                return [("q", 1, i) for i in range(2 * NCH)] + [("unit", 1, i) for i in range(2 * U)] + \
                    [("row", 1, i) for i in range(NCH)]
            uses = []
            for place, made in sorted(fill_of(g).items()):
                for kind, rel, n in made:
                    uses += [(kind, rel, i) for i in range(NB)] if kind == "proj" else [(kind, rel, n)]
            return uses

        STAGES = 4

        def steps_after(uses):
            steps = {n: [] for n in range(len(uses))}
            for n, (kind, rel, i) in enumerate(uses):
                later = [m for m in range(n + 1, len(uses)) if uses[m][0] in ("q", "unit")]
                if kind == "den":
                    for k in range(STAGES):
                        steps[later[k] if len(later) >= STAGES else n].append(("den", rel, i, k + 1))
                if kind == "unit" and i % U == U - 1:
                    steps[n].append(("max", rel, i // U, 0))
                    for k in range(2):
                        steps[later[k] if len(later) >= 2 else n].append(("max", rel, i // U, k + 1))
            return steps

        def banks_of(g):
            start = 0
            for k in range(-1, g):
                start += len(uses_of(k))
            return {u: (start + n) % 2 for n, u in enumerate(uses_of(g))}

        def bank_of(g, use):
            kind, rel, i = use
            if g < 0:
                return scores[:, i // 2 % 2, i % 2, :] if kind == "unit" else misc[:, i % 2, :]
            return misc[:, banks_of(g)[use], :]

        def all_pairs(eng, body):
            for b in range(B):
                body(b * PAIRS, b * PAIRS, b)
                with eng.Fori(0, (PAIRS - 2) // 2) as i:
                    for k in (1, 2):
                        body(2 * i + (b * PAIRS + k), b * PAIRS + 2 + k, b)
                body((b + 1) * PAIRS - 1, (b + 1) * PAIRS - 1, b)

        SQRT_TILE = 4

        pieces = [(0, P), (P, P), (2 * P, HID - 2 * P)]
        shared_pieces = [(0, P), (P, SHID - P)]
        E_LOADS = 16 * 4

        def pieces_of(s):
            return pieces if s else shared_pieces

        def units_before(number):
            if isinstance(number, int) and number == 0:
                return 0
            return len(shared_pieces) * NJ + len(pieces) * NJ * (number - 1)

        def all_experts(eng, body):
            for s in range(3):
                body(s, s)
            with eng.Fori(0, (E - 4) // 2) as i:
                for k in (3, 4):
                    body(2 * i + k, k)
            for s in (E - 1, E):
                body(s, s)

        @block.sync
        def _(sp):
            for t0 in range(0, NT, 4):
                sp.dma_start(x_sb[:, t0:t0 + 4, :],
                             x.rearrange("b n d -> (b n) d").rearrange("(t p) d -> p t d", p=P)[:, t0:t0 + 4, :]
                             ).then_inc(x_loaded[t0 // 4], 16)
            sp.dma_start(ident[:], ident_f).then_inc(ident_loaded, 16)
            sp.dma_start(wq_raw, wq).then_inc(w_loaded, 16)
            for j in range(2):
                sp.dma_start(wkv_raw[:, j, :], wkv).then_inc(w_loaded, 16)
            sp.dma_start(null_bc[:], null_kv.rearrange("(a d) -> a d", a=1).broadcast_to([P, DH])
                         ).then_inc(null_loaded, 16)
            for j in range(2):
                sp.dma_start(null_col[j * DH:(j + 1) * DH, :], null_kv.rearrange("(d a) -> d a", a=1)
                             ).then_inc(null_loaded, 16)
            for b in range(B):
                sp.dma_start(kf[:, b, 0:1], null_kv.rearrange("(d a) -> d a", a=1)).then_inc(null_loaded, 16)
            for dst, src in ((identb, ident_b), (maskt, mask_t), (maskn, mask_n), (maskf, mask_fix)):
                sp.dma_start(dst[:], src).then_inc(c_loaded, 16)
            sp.dma_start(wout_sb[:], wout.rearrange("(p k) n -> k p n", k=P)).then_inc(wout_loaded, 16)
            sp.dma_start(gate_raw[:], gate_w).then_inc(g_loaded, 16)

            sp.wait_ge(v_turned, B + 1)
            sp.wait_ge(kv_low, B * NCH + B)

            def body(number, s):
                k = s % 2
                if s >= 2:
                    sp.wait_ge(down_filled, NJ * (number - 1))
                if s == 0:
                    srcs, hid = (sw1, sw3, sw2), SHID
                else:
                    e = number - 1
                    srcs = tuple(w[bass.ds(e, 1), :, :].rearrange("o a b -> (o a) b") for w in (w1, w3, w2))
                    hid = HID
                for j in range(2):
                    sp.dma_start(up_raw[:, k, j, 0:hid], srcs[j]).then_inc(ew_loaded[k], 16)
                whole = hid // P
                sp.dma_start(down_w[:, k, 0:whole, :],
                             srcs[2][0:whole * P, :].rearrange("(c p) d -> p c d", p=P)).then_inc(ew_loaded[k], 16)
                sp.dma_start(down_w[0:hid - whole * P, k, whole, :], srcs[2][whole * P:hid, :]
                             ).then_inc(ew_loaded[k], 16)

            all_experts(sp, body)
            for q in range(4):
                sp.wait_ge(result_ready, q + 1)
                sp.dma_start(out.rearrange("b n d -> (b n) d").rearrange("(t p) d -> p t d", p=P)[:, 4 * q:4 * q + 4, :],
                             xn[:, 4 * q:4 * q + 4, :]).then_inc(stored, 16)
            sp.wait_ge(stored, 16 * 4)

        W_LOADS, NULL_LOADS, C_LOADS = 16 * 3, 16 * (3 + B), 16 * 4
        WQ = HEADS * DH
        FIX = NT * HEADS

        @block.gpsimd
        def _(pool):
            pool.wait_ge(w_loaded, W_LOADS)
            pool.tensor_scalar(wq_scaled, wq_raw, SCALE, None, ALU.mult).then_inc(w_scaled, 1)
            pool.wait_ge(w_scaled, 1)
            pool.wait_ge(w_high, 2)
            pool.tensor_tensor(wq_lo[:, 0:WQ], wq_scaled, wq_hi[:, 0:WQ].bitcast(F32), ALU.subtract).then_inc(w_low, 1)
            pool.tensor_tensor(wq_lo[:, WQ:WQ + P], wq_scaled[:, 0:P], wq_hi[:, 0:P].bitcast(F32), ALU.subtract
                               ).then_inc(w_low, 1)
            pool.wait_ge(null_loaded, NULL_LOADS)
            pool.tensor_tensor(wn_prod, wq_scaled.rearrange("p (h d) -> p h d", d=DH),
                               null_bc[:].unsqueeze(1).broadcast_to([P, HEADS, DH]), ALU.mult
                               ).then_inc(wn_multiplied, 1)
            pool.memset(ones[:], 1.0)
            pool.memset(m_part[:], LOWEST)
            pool.memset(row_sel[:, 0:DH].bitcast(F32), 0.0)
            pool.memset(row_sel[:, DH:DH + 1].bitcast(F32), 1.0).then_inc(consts_ready, 1)
            pool.wait_ge(consts_ready, 1)
            pool.memset(k_lo[DH:DH + 1, :, :].bitcast(F32), 1.0).then_inc(consts_ready, 1)
            pool.wait_ge(ident_loaded, 16)
            pool.wait_ge(consts_ready, 2)
            pool.tensor_scalar(neg_ident[:], ident[:], -1.0, None, ALU.mult).then_inc(consts_ready, 1)

            def split_weights(number, s):
                k, hid = s % 2, HID if s else SHID
                pool.wait_ge(ew_loaded[k], (number - k) * (E_LOADS // 2) + E_LOADS)
                if s >= 2:
                    pool.wait_ge(up_filled, units_before(number - 1))
                pool.tensor_tensor(up_hi[:, k, :, 0:hid], up_raw[:, k, :, 0:hid],
                                   ones[:, 0:1].unsqueeze(2).broadcast_to([P, 2, hid]), ALU.mult).then_inc(ew_high, 1)
                pool.wait_ge(ew_high, number + 1)
                pool.tensor_tensor(up_lo[:, k, :, 0:hid], up_raw[:, k, :, 0:hid], up_hi[:, k, :, 0:hid].bitcast(F32),
                                   ALU.subtract).then_inc(ew_split, 1)

            def body(number, g, b):
                if g == B * PAIRS - 1:
                    for s in range(2):
                        split_weights(s, s)
                for t in range(1, T):
                    if t not in summed_after:
                        continue
                    c, kb, first = tiles[t]
                    t0 = first_of[c]
                    slot = (t - 1) % NPB
                    if t == t0:
                        continue
                    pool.wait_ge(probs_ready, T * number + t + 1)
                    acc = psums[:, c, :, :]
                    if t == t0 + 1:
                        if g > 0:
                            pool.wait_ge(den_filled, NCH * (number - 1) + c + 1)
                        before = probs[:, (t0 - 1) % NPB, :, :]
                        pool.tensor_tensor(acc[:, :, first:CH], before[:, :, first:CH], probs[:, slot, :, first:CH],
                                           ALU.add).then_inc(summed, 1 if first else 2)
                        if first:
                            pool.tensor_scalar(acc[:, :, 0:first], before[:, :, 0:first], 1.0, None, ALU.mult
                                               ).then_inc(summed, 1)
                    else:
                        pool.wait_ge(summed, SUMS * number + summed_after[t] - 1)
                        pool.tensor_tensor(acc[:, :, first:CH], acc[:, :, first:CH], probs[:, slot, :, first:CH],
                                           ALU.add).then_inc(summed, 1)
                    if t == last_of[c] - NARROW:
                        pool.wait_ge(summed, SUMS * number + summed_after[t])
                        pool.tensor_tensor(acc[0:2, :, CH - 1], acc[0:2, :, CH - 1], probs_fix[:, g % 2, :, c],
                                           ALU.add).then_inc(sums_ready, 1)

            all_pairs(pool, body)

            def split_later(number, s):
                if s >= 2:
                    split_weights(number, s)

            all_experts(pool, split_later)

        @block.scalar
        def _(act):
            def deviations(n, first, tiles):
                act.wait_ge(var_ready, n)
                act.activation(std[:, first:first + tiles], vare[:, first:first + tiles], ACT.Sqrt
                               ).then_inc(sqrt_done, 1)

            def high_tokens(n, j, bank):
                act.wait_ge(turned, n * NJ + j + 1)
                act.activation(xt_hi[:, j * CH:(j + 1) * CH], bank, ACT.Copy).then_inc(t_high, 1)

            def weights(pair):
                for dst, src in ((wcur_hi, wq_hi), (wcur_lo, wq_lo)):
                    for j in range(2):
                        act.activation(dst[:, :, j, :],
                                       src[:, bass.ds(pair * P, P)].bitcast(F32).rearrange("p (h d) -> p h d", h=2),
                                       ACT.Copy).then_inc(wcur_ready, 1)

            def high_part(number, g, i):
                par, bank = (g + 1) % 2, bank_of(g, ("q", 1, i))
                h, c = divmod(i, NCH)
                act.wait_ge(q_filled, PER_PAIR["q"] * (number + 1) + i + 1)
                if i == 0 and g >= 1:
                    act.wait_ge(scores_ready, T * number)
                act.activation(q_split[0:DH, par, h, c * CH:(c + 1) * CH], bank[0:DH, :], ACT.Copy
                               ).then_inc(q_copied, 1)
                act.activation(q_hi[:, par, h, c * CH:(c + 1) * CH], bank, ACT.Copy).then_inc(q_high, 1)

            def copy_row(number, g, rel, i):
                h, c = divmod(i, NCH)
                act.wait_ge(row_filled, PER_PAIR["row"] * (number + rel) + i + 1)
                act.activation(q_hi[DH:DH + 1, (g + rel) % 2, h, c * CH:(c + 1) * CH],
                               bank_of(g, ("row", rel, i))[DH:DH + 1, :], ACT.Copy).then_inc(row_copied, 1)

            def copy_keys(b):
                for c in range(NCH):
                    act.wait_ge(kv_filled, b * NCH + c + 1)
                    act.activation(k_hi[:, b, 1 + c * CH:1 + (c + 1) * CH], scores[:, b, c, :], ACT.Copy
                                   ).then_inc(kv_high, 1)
                    act.activation(kf[:, b, 1 + c * CH:1 + (c + 1) * CH], scores[0:DH, b, c, :], ACT.Copy
                                   ).then_inc(kv_copied, 1)

            deviations(1, 0, NB)
            act.wait_ge(w_loaded, W_LOADS)
            act.activation(wkv_hi[:], wkv_raw[:], ACT.Copy).then_inc(wkv_high, 1)
            act.activation(wq_hi[:, 0:WQ], wq_raw, ACT.Copy, scale=SCALE).then_inc(w_high, 1)
            act.activation(wq_hi[:, WQ:WQ + P], wq_raw[:, 0:P], ACT.Copy, scale=SCALE).then_inc(w_high, 1)

            for j in range(NCH):
                high_tokens(0, j, scores[:, 0, j, :])
            deviations(2, NB, NB)
            act.wait_ge(w_high, 2)
            act.wait_ge(w_low, 2)
            weights(0)
            copy_keys(0)
            for j in range(NCH):
                high_tokens(0, NCH + j, scores[:, 1, j, :])
            for i in range(2 * NCH):
                high_part(-1, -1, i)
            copy_keys(1)
            act.wait_ge(null_loaded, NULL_LOADS)
            for b in range(B):
                act.activation(k_hi[:, b, 0:1], null_col[:], ACT.Copy).then_inc(kv_high, 1)
            weights(1)
            for b in range(B):
                act.wait_ge(null_filled, b + 1)
                if b == B - 1:
                    act.wait_ge(v_turned, 1)
                act.activation(s_null[:, b * NB:(b + 1) * NB, :],
                               o_ps[:, 0, b * NB * HEADS:(b + 1) * NB * HEADS].rearrange("p (t h) -> p t h", h=HEADS),
                               ACT.Copy).then_inc(null_copied, 1)
            act.activation(v_fix[:], o_ps[0:2, 0, FIX:FIX + B * DH].rearrange("p (b d) -> p b d", b=B), ACT.Copy
                           ).then_inc(v_copied, 1)
            for n, b in enumerate(reversed(range(B))):
                act.wait_ge(v_turned, n + 2)
                act.activation(v_sb[:, b, :, :], o_ps[:, b, :].rearrange("p (k d) -> p k d", d=DH), ACT.Copy
                               ).then_inc(v_copied, 1)
            for i in range(NCH):
                copy_row(-1, -1, 1, i)

            def body(number, g, b):
                fill = fill_of(g)

                def filled(place):
                    for kind, rel, i in fill.get(place, []):
                        if kind == "q":
                            high_part(number, g, i)
                            if i == 2 * NCH - 1 and g + 2 < B * PAIRS:
                                weights(number + 2 - b * PAIRS if g % PAIRS < PAIRS - 1 else 1)
                        elif kind == "row":
                            copy_row(number, g, rel, i)
                        elif kind == "proj":
                            for k in range(NB):
                                project_copy(k, banks_of(g)["proj", 0, k])
                        elif kind == "part":
                            project_copy(NB + i, banks_of(g)["part", 0, i])

                filled((-1, 0))
                for t in range(T):
                    st = (g * T + t) % 2
                    if t:
                        filled((t - 1, 0))
                    act.wait_ge(scores_ready, T * number + t + 1)
                    if t == 0:
                        act.activation(probs_fix[:, g % 2, :, :], scores[0:2, st, :, 0:2], ACT.Exp
                                       ).then_inc(probs_ready, 1)
                        continue
                    c, kb, first = tiles[t]
                    slot = (t - 1) % NPB
                    if t > NPB or g > 0:
                        old, of = (t - NPB, number) if t > NPB else (TF + t - NPB, number - 1)
                        act.wait_ge(av_done, TF * of + old)
                        if old in summed_after:
                            act.wait_ge(summed, SUMS * of + summed_after[old])
                        else:
                            act.wait_ge(den_filled, NCH * of + tiles[old][0] + 1)
                    act.activation(probs[:, slot, :, first:CH], scores[:, st, :, first:CH], ACT.Exp
                                   ).then_inc(probs_ready, 1)
                    filled((t - 1, 1))
                    filled((t - 1, 2))
                    if g == B * PAIRS - 1 and t == SQRT_TILE:
                        deviations(3, 0, NB)
                filled((TF, 2))

            def project_copy(i, bank):
                act.wait_ge(proj_filled, i + 1)
                act.activation(attn[:, i, :], misc[:, bank, 0:D], ACT.Copy).then_inc(proj_copied, 1)

            all_pairs(act, body)
            deviations(4, 0, NB)
            deviations(5, NB, BPC)
            for j in range(NCH):
                high_tokens(1, j, scores[:, 0, j, :])

            def silu(number, s):
                for j in range(NJ):
                    for i, (_, rows_) in enumerate(pieces_of(s)):
                        n = j * len(pieces_of(s)) + i
                        at = units_before(number) + n
                        act.wait_ge(up_filled, at + 1)
                        if s or n >= 2:
                            act.wait_ge(hidden_ready, at - 1)
                        act.activation(gated[0:rows_, n % 2, :], scores[0:rows_, n % 2, 0, :], ACT.Silu
                                       ).then_inc(silu_done, 1)
                    if s == 0 and j == 0:
                        deviations(6, NB + BPC, BPC)
                        deviations(7, NB, BPC)
                    if s == 0 and j == 1:
                        high_tokens(1, 2, misc[:, 0, :])
                        deviations(8, NB + BPC, BPC)
                    if s == 0 and j == 2:
                        high_tokens(1, 3, misc[:, 0, :])
                if s == 0:
                    act.wait_ge(logits_copied, 1)
                    act.activation(rest[:], logits[:], ACT.Exp).then_inc(exp_done, 1)

            all_experts(act, silu)
            for j in range(NJ):
                deviations(9 + j, j * BPC, BPC)

        @block.tensor
        def _(pe):
            pe.wait_ge(ident_loaded, 16)

            def turn_tokens(n, j, bank):
                for k in range(BPC):
                    t = j * BPC + k
                    pe.wait_ge(norm_done, n * NT + t + 1)
                    mm = pe.transpose(bank[:, k * P:(k + 1) * P], xn[:, t, :], ident[:])
                mm.then_inc(turned, 1)

            for j in range(NCH):
                turn_tokens(0, j, scores[:, 0, j, :])
            pe.wait_ge(wkv_high, 1)
            pe.wait_ge(wkv_low, 1)

            def keys(b):
                for j in range(b * NCH, (b + 1) * NCH):
                    pe.wait_ge(t_high, j + 1)
                    pe.wait_ge(t_low, j + 1)
                    dst = scores[:, b, j % NCH, :]
                    sl = slice(j * CH, (j + 1) * CH)
                    pe.matmul(dst, wkv_hi[:].rearrange("p a d -> p (a d)"), xt_hi[:, sl], start=True, stop=False)
                    pe.matmul(dst, wkv_lo[:].rearrange("p a d -> p (a d)"), xt_hi[:, sl], start=False, stop=False)
                    pe.matmul(dst, wkv_hi[:].rearrange("p a d -> p (a d)"), xt_lo[:, sl], start=False, stop=True
                              ).then_inc(kv_filled, 1)

            keys(0)

            def null_products(t):
                pe.wait_ge(wn_split, 2)
                dst = o_ps[:, 0, t * HEADS:(t + 1) * HEADS]
                sl = slice(t * P, (t + 1) * P)
                pe.matmul(dst, xt_hi[:, sl], wn_hi[:], start=True, stop=False)
                pe.matmul(dst, xt_hi[:, sl], wn_lo[:], start=False, stop=False)
                mm = pe.matmul(dst, xt_lo[:, sl], wn_hi[:], start=False, stop=True)
                if t % NB == NB - 1:
                    mm.then_inc(null_filled, 1)

            def leftover_values():
                pe.wait_ge(kv_copied, B * NCH)
                pe.wait_ge(null_loaded, NULL_LOADS)
                for b in range(B):
                    mm = pe.transpose(o_ps[0:2, 0, FIX + b * DH:FIX + (b + 1) * DH], kf[:, b, CH:N + 1:CH],
                                      ident[0:DH, 0:DH])
                mm.then_inc(v_turned, 1)

            def turn_values(b, quarter):
                if (b, quarter) == (0, 0):
                    pe.wait_ge(null_copied, B)
                    pe.wait_ge(v_copied, 1)
                for kb in range(quarter * NB // 4, (quarter + 1) * NB // 4):
                    mm = pe.transpose(o_ps[:, b, kb * DH:(kb + 1) * DH], kf[:, b, kb * P:(kb + 1) * P],
                                      ident[0:DH, 0:DH])
                if quarter == 3:
                    mm.then_inc(v_turned, 1)

            def take(g, number, kind, state):
                seq_before = uses_of(g - 1) if g >= 0 else []
                mine = uses_of(g)
                n = state[0]
                state[0] += 1
                assert mine[n][0] == kind, (mine[n], kind)
                if g < 0:
                    i = mine[n][2]
                    if kind == "q" and i >= 2:
                        pe.wait_ge(q_low, i - 1)
                    if kind == "unit" and i >= 4:
                        pe.wait_ge(unit_max, i - 3)
                    if kind == "row":
                        pe.wait_ge(q_low, 2 * NCH - 1 + i)
                    return bank_of(g, mine[n])
                seq = [(u, -1) for u in seq_before] + [(u, 0) for u in mine]
                at = len(seq_before) + n
                if at >= 2:
                    (k, rel, i), pair = seq[at - 2]
                    if k in ("proj", "part"):
                        pe.wait_ge(proj_copied, (NB if k == "part" else 0) + i + 1)
                    else:
                        pe.wait_ge(READ_BY[k], PER_PAIR[k] * (number + rel + pair) + i + 1)
                return bank_of(g, mine[n])

            def queries(g, number, i, state):
                nb = (g + 1) // PAIRS
                if i == 0:
                    pe.wait_ge(wcur_ready, 4 * (number + 2))
                h, c = divmod(i, NCH)
                dst = take(g, number, "q", state)
                sl = slice(nb * N + c * CH, nb * N + (c + 1) * CH)
                hi = wcur_hi[:, h, :, :].rearrange("p a d -> p (a d)")
                lo = wcur_lo[:, h, :, :].rearrange("p a d -> p (a d)")
                pe.matmul(dst, hi, xt_hi[:, sl], start=True, stop=False)
                pe.matmul(dst, hi, xt_lo[:, sl], start=False, stop=False)
                pe.matmul(dst, lo, xt_hi[:, sl], start=False, stop=True).then_inc(q_filled, 1)

            def maximum_unit(g, number, i, state):
                nb, par = (g + 1) // PAIRS, (g + 1) % 2
                h, u = divmod(i, U)
                qb, kc, n = units[u]
                if u == 0:
                    pe.wait_ge(q_low, PER_PAIR["q"] * (number + 1) + NCH * (h + 1))
                    pe.wait_ge(q_copied, PER_PAIR["q"] * (number + 1) + NCH * (h + 1))
                dst = take(g, number, "unit", state)
                diagonal = kc == qb // BPC
                mm = pe.matmul(dst[:, 0:n], q_split[:, par, h, qb * P:(qb + 1) * P],
                               k_hi[:, nb, 1 + kc * CH:1 + kc * CH + n], start=True, stop=True)
                if diagonal:
                    mm = pe.matmul(dst[:, n - P:n], identb[:], maskn[:], start=False, stop=True,
                               skip_group_check=True)
                mm.then_inc(unit_filled, 1)

            def row(g, number, rel, i, state):
                h, c = divmod(i, NCH)
                pe.wait_ge(spread_ready, PER_PAIR["row"] * (number + rel) + i + 1)
                dst = take(g, number, "row", state)
                pe.matmul(dst[0:DH + 1, :], row_sel[:],
                          spread[:, h, c * BPC:(c + 1) * BPC, :].rearrange("p b q -> p (b q)"),
                          start=True, stop=True).then_inc(row_filled, 1)

            def score(g, number, t, b, h):
                st, par = (g * T + t) % 2, g % 2
                use = T * number + t
                if h == 0 and (t >= 2 or g > 0):
                    pe.wait_ge(probs_ready, use - 1)
                if t == 0:
                    qs, ks = slice(CH - 1, N, CH), slice(CH, N + 1, CH)
                    dst = scores[0:2, st, h, 0:2]
                else:
                    c, kb, first = tiles[t]
                    qs, ks = slice(c * CH + first, (c + 1) * CH), slice(kb * P, (kb + 1) * P)
                    dst = scores[:, st, h, first:CH]
                mm = pe.matmul(dst, k_hi[:, b, ks], q_split[:, par, h, qs], start=True, stop=False)
                if t == 0 or (t, h) == (1, 0):
                    pe.wait_ge(row_copied, PER_PAIR["row"] * number + NCH * (h + 1))
                mm = pe.matmul(dst, k_lo[:, b, ks], q_hi[0:DH + 1, par, h, qs], start=False, stop=True)
                if t == 0:
                    mm = pe.matmul(dst, identb[0:2, 0:2], maskf[:], start=False, stop=True, skip_group_check=True)
                elif kb * P - 2 + P > c * CH:
                    skip = 0 if first else 2
                    m0 = P * kb - 2 + skip - CH * c
                    w = P + 2 - skip
                    mm = pe.matmul(scores[:, st, h, m0:m0 + w], identb[:], maskt[:, skip:skip + w],
                                   start=False, stop=True, skip_group_check=True)
                if h == 1:
                    mm.then_inc(scores_ready, 1)

            def weigh(g, number, t, b):
                c, kb, first = tiles[t]
                pe.wait_ge(probs_ready, T * number + t + 1)
                if t == first_of[0] and g == 0:
                    pe.wait_ge(gate_split, 1)
                if t == first_of[c] and g > 0:
                    pe.wait_ge(o_done, NCH * (number - 1) + c + 1)
                slot = (t - 1) % NPB
                for h in range(2):
                    mm = pe.matmul(o_ps[h * DH:(h + 1) * DH, c, first:CH], v_sb[:, b, kb, :],
                                   probs[:, slot, h, first:CH], start=t == first_of[c], stop=t == last_of[c],
                                   skip_group_check=True)
                    if t == first_of[c]:
                        mm = pe.matmul(o_ps[h * DH:(h + 1) * DH, c, CH - 1:CH], v_fix[:, b, :],
                                       probs_fix[:, g % 2, h, c:c + 1], start=False, stop=False,
                                       skip_group_check=True)
                mm.then_inc(av_done, 1)

            def denominators(g, number, c, rel, state):
                pe.wait_ge(sums_ready, NCH * (number + rel) + c + 1)
                pe.wait_ge(probs_ready, T * (number + rel) + last_of[c] + 1)
                dst = take(g, number, "den", state) if state is not None else misc[:, 0, :]
                for h in range(2):
                    rows_ = slice(h * DH, (h + 1) * DH)
                    mm = pe.matmul(dst[rows_, :], ones[:], psums[:, c, h, :], start=True, stop=True,
                                   skip_group_check=True)
                    for t in range(last_of[c] - NARROW + 1, last_of[c] + 1):
                        first = tiles[t][2]
                        mm = pe.matmul(dst[rows_, first:CH], ones[:], probs[:, (t - 1) % NPB, h, first:CH],
                                       start=False, stop=True, skip_group_check=True)
                mm.then_inc(den_filled, 1)

            def project(g, number, kind, i, state):
                b, pairs = (0, PAIRS) if kind == "proj" else (B - 1, PAIRS - 1)
                pe.wait_ge(o_done, NCH * (PAIRS * b + pairs))
                dst = take(g, number, kind, state)
                for p in range(pairs):
                    mm = pe.matmul(dst[:, 0:D], heads_out[:, p, i * P:(i + 1) * P], wout_sb[:, p, :],
                                   start=p == 0, stop=p == pairs - 1)
                mm.then_inc(proj_filled, 1)

            def project_rest(c, bank):
                pe.wait_ge(o_done, NCH * (B * PAIRS - 1) + c + 1)
                for i in range(BPC):
                    mm = pe.matmul(bank[:, i * D:(i + 1) * D],
                                   heads_out[:, PAIRS - 1, (c * BPC + i) * P:(c * BPC + i + 1) * P],
                                   wout_sb[:, PAIRS - 1, :], start=True, stop=True)
                mm.then_inc(rest_filled, 1)

            state = [0]
            for i in range(NCH):
                queries(-1, -1, i, state)
            for j in range(NCH):
                turn_tokens(0, NCH + j, scores[:, 1, j, :])
            for t in range(NB):
                null_products(t)
            for i in range(NCH, 2 * NCH):
                queries(-1, -1, i, state)
            keys(1)
            pe.wait_ge(consts_ready, 3)
            pe.wait_ge(c_loaded, C_LOADS)
            pe.wait_ge(kv_low, B * NCH + B)
            pe.wait_ge(kv_high, B * NCH + B)
            for i in range(2 * U):
                if i == 4:
                    pe.wait_ge(null_copied, 1)
                if 4 <= i < 4 + NB:
                    null_products(NB + i - 4)
                if i == U:
                    leftover_values()
                if i > U and (i - U - 1) // 4 < B:
                    turn_values(B - 1 - (i - U - 1) // 4, (i - U - 1) % 4)
                maximum_unit(-1, -1, i, state)
            for i in range(NCH):
                row(-1, -1, 1, i, state)
            pe.wait_ge(g_loaded, 16)
            pe.wait_ge(v_copied, B + 1)
            pe.transpose(o_ps[:, 0, 0:E], gate_raw[:], ident[0:E, 0:E]).then_inc(gate_turned, 1)
            pe.wait_ge(unit_max, 2 * U)
            pe.wait_ge(wout_loaded, 16)

            def body(number, g, b):
                state = [0]
                fill = fill_of(g)

                def make(place):
                    for kind, rel, i in fill.get(place, []):
                        if kind == "q":
                            queries(g, number, i, state)
                        elif kind == "unit":
                            maximum_unit(g, number, i, state)
                        elif kind == "den":
                            denominators(g, number, i, rel, state)
                        elif kind == "row":
                            row(g, number, rel, i, state)
                        elif kind == "proj":
                            for k in range(NB):
                                project(g, number, kind, k, state)
                        elif kind == "rest":
                            project_rest(0, take(g, number, kind, state))
                        else:
                            project(g, number, kind, i, state)

                score(g, number, 1, b, 0)
                make((-1, 0))
                for h in range(2):
                    score(g, number, 0, b, h)
                for t in range(T):
                    if 0 < t < T - 1:
                        score(g, number, t + 1, b, 0)
                    make((t, 0))
                    if t + 1 < T:
                        score(g, number, t + 1, b, 1)
                    make((t, 1))
                    if t:
                        weigh(g, number, t, b)
                    make((t, 2))
                if g == B * PAIRS - 1:
                    pe.wait_ge(den_turned, NCH * number + 1)
                    pe.wait_ge(proj_copied, B * NB)
                    pe.wait_ge(rest_added, 1)
                    denominators(g, number, 1, 0, None)

            all_pairs(pe, body)

            def logit_products(b):
                for t in range(b * NB, (b + 1) * NB):
                    sl = slice(t * P, (t + 1) * P)
                    dst = misc[:, 1, t * E:(t + 1) * E]
                    pe.matmul(dst, xt_hi[:, sl], gate_hi[:], start=True, stop=False)
                    pe.matmul(dst, xt_hi[:, sl], gate_lo[:], start=False, stop=False)
                    mm = pe.matmul(dst, xt_lo[:, sl], gate_hi[:], start=False, stop=True)
                mm.then_inc(logits_filled, 1)

            pe.wait_ge(probs_ready, T * B * PAIRS)
            for j in range(NCH):
                turn_tokens(1, j, scores[:, 0, j, :])

            def up(number, s, j, i):
                k, sl = s % 2, slice(j * CH, (j + 1) * CH)
                r0, rows_ = pieces_of(s)[i]
                n = j * len(pieces_of(s)) + i
                at = units_before(number) + n
                if s or n >= 2:
                    pe.wait_ge(hidden_ready, at - 1)
                for m in range(2):
                    dst = scores[0:rows_, n % 2, m, :]
                    hi, lo = up_hi[:, k, m, r0:r0 + rows_], up_lo[:, k, m, r0:r0 + rows_]
                    pe.matmul(dst, hi, xt_hi[:, sl], start=True, stop=False)
                    pe.matmul(dst, hi, xt_lo[:, sl], start=False, stop=False)
                    mm = pe.matmul(dst, lo, xt_hi[:, sl], start=False, stop=True)
                mm.then_inc(up_filled, 1)

            def down(number, s, j, half):
                k, ps = s % 2, pieces_of(s)
                if half == 0:
                    pe.wait_ge(hidden_ready, units_before(number) + (j + 1) * len(ps))
                    if s or j >= 2:
                        pe.wait_ge(added, NJ * number + j - 1)
                for t in range(half * BPC // 2, (half + 1) * BPC // 2):
                    for i, (_, rows_) in enumerate(ps):
                        mm = pe.matmul(o_ps[:, j % 2, t * P:(t + 1) * P], hidden[0:rows_, j % 2, i, t * P:(t + 1) * P],
                                       down_w[0:rows_, k, i, :], start=i == 0, stop=i == len(ps) - 1)
                if half:
                    mm.then_inc(down_filled, 1)

            def experts(number, s):
                pe.wait_ge(ew_split, number + 1)
                for j in range(NJ):
                    if s == 0 and j == 2:
                        pe.wait_ge(rest_added, NCH)
                        turn_tokens(1, j, misc[:, 0, :])
                    if s == 0:
                        pe.wait_ge(t_low, NJ + max(j + 1, NCH))
                        pe.wait_ge(t_high, NJ + max(j + 1, NCH))
                    before = (number, s, j - 1) if j else (number - 1, 0 if s == 1 else s - 1, NJ - 1) if s else None
                    for i in range(len(pieces_of(s))):
                        up(number, s, j, i)
                        if i and before:
                            down(*before, i - 1)
                    if len(pieces_of(s)) == 2 and before:
                        down(*before, 1)
                    if s == 0 and j == 1:
                        logit_products(0)
                    if s == 0 and j == 0:
                        pe.wait_ge(den_turned, NCH * PAIRS * B)
                        project_rest(1, misc[:, 0, :])
                    if s == 0 and j == 2:
                        turn_tokens(1, j + 1, misc[:, 0, :])
                    if s == 0 and j == 3:
                        logit_products(1)

            all_experts(pe, experts)
            for half in range(2):
                down(E, E, NJ - 1, half)

        @block.vector
        def _(dve):
            steps = [0]

            def link(ins):
                steps[0] += 1
                ins.then_inc(vec, 1)
                dve.wait_ge(vec, steps[0])

            def variances(src, tiles, loads=False):
                for t in tiles:
                    if loads and t % 4 == 0:
                        dve.wait_ge(x_loaded[t // 4], 16)
                    done = dve.bn_stats(stats[:, t, :], src[:, t, :])
                link(done)
                for t in tiles:
                    done = dve.bn_aggr(mv[:, t, :], stats[:, t, :])
                link(done)
                sl = slice(tiles[0], tiles[-1] + 1)
                dve.tensor_scalar(vare[:, sl], mv[:, sl, 1], EPS, None, ALU.add).then_inc(var_ready, 1)

            def normalize_tokens(n, dst, src, tiles):
                sl = slice(tiles[0], tiles[-1] + 1)
                dve.wait_ge(sqrt_done, n)
                link(dve.reciprocal(rstd[:, sl], std[:, sl]))
                for t in tiles:
                    done = dve.tensor_scalar(dst[:, t, :], src[:, t, :], mv[:, t, 0:1], rstd[:, t:t + 1],
                                             ALU.subtract, ALU.mult)
                    if dst is xn and src is x_sb:
                        done.then_inc(norm_done, 1)
                return done

            def add_attention(n, tiles):
                link(normalize_tokens(n, xn, attn, tiles))
                sl = slice(tiles[0], tiles[-1] + 1)
                link(dve.tensor_tensor(x_sb[:, sl, :], x_sb[:, sl, :], xn[:, sl, :], ALU.add))
                variances(x_sb, tiles)

            def low_tokens(n, j, bank):
                dve.wait_ge(t_high, n * NJ + j + 1)
                dve.tensor_tensor(xt_lo[:, j * CH:(j + 1) * CH], bank, xt_hi[:, j * CH:(j + 1) * CH].bitcast(F32),
                                  ALU.subtract).then_inc(t_low, 1)

            variances(x_sb, range(NB), loads=True)
            normalize_tokens(1, xn, x_sb, range(NB))
            dve.wait_ge(wkv_high, 1)
            dve.tensor_tensor(wkv_lo[:], wkv_raw[:], wkv_hi[:].bitcast(F32), ALU.subtract).then_inc(wkv_low, 1)
            for j in range(NCH):
                low_tokens(0, j, scores[:, 0, j, :])
            variances(x_sb, range(NB, NT), loads=True)
            normalize_tokens(2, xn, x_sb, range(NB, NT))
            dve.wait_ge(wn_multiplied, 1)
            link(dve.tensor_reduce(wn[:], wn_prod, AX_X, ALU.add))
            dve.tensor_copy(wn_hi[:], wn[:]).then_inc(wn_split, 1)
            dve.wait_ge(wn_split, 1)
            dve.tensor_tensor(wn_lo[:], wn[:], wn_hi[:].bitcast(F32), ALU.subtract).then_inc(wn_split, 1)

            def low_keys(b):
                for c in range(NCH):
                    sl = slice(1 + c * CH, 1 + (c + 1) * CH)
                    dve.wait_ge(kv_high, b * NCH + c + 1)
                    dve.wait_ge(kv_copied, b * NCH + c + 1)
                    dve.tensor_tensor(k_lo[0:DH, b, sl], scores[0:DH, b, c, :], k_hi[0:DH, b, sl].bitcast(F32),
                                      ALU.subtract).then_inc(kv_low, 1)

            def low_part(g, number, i):
                par, bank = (g + 1) % 2, bank_of(g, ("q", 1, i))
                h, c = divmod(i, NCH)
                sl = slice(c * CH, (c + 1) * CH)
                dve.wait_ge(q_high, PER_PAIR["q"] * (number + 1) + i + 1)
                dve.tensor_tensor(q_split[DH:P, par, h, sl], bank[DH:P, :],
                                  q_hi[DH:P, par, h, sl].bitcast(F32), ALU.subtract).then_inc(q_low, 1)

            low_keys(0)
            for j in range(NCH):
                low_tokens(0, NCH + j, scores[:, 1, j, :])
            for i in range(2 * NCH):
                low_part(-1, -1, i)
            low_keys(1)
            dve.wait_ge(kv_high, B * NCH + B)
            for b in range(B):
                dve.tensor_tensor(k_lo[0:DH, b, 0:1], kf[:, b, 0:1], k_hi[0:DH, b, 0:1].bitcast(F32), ALU.subtract
                                  ).then_inc(kv_low, 1)

            def unit(g, number, i):
                h, u = divmod(i, U)
                qb, kc, n = units[u]
                bank = bank_of(g, ("unit", 1, i))
                dve.wait_ge(unit_filled, PER_PAIR["unit"] * (number + 1) + i + 1)
                dve.tensor_reduce(m_part[:, h, qb, kc:kc + 1], bank[:, 0:n], AX_X, ALU.max
                                  ).then_inc(unit_max, 1)

            def whole_max(g, number, h, stage):
                nb = (g + 1) // PAIRS
                head = 2 * (number + 1 - nb * PAIRS) + h
                if stage == 0:
                    dve.wait_ge(unit_max, PER_PAIR["unit"] * (number + 1) + (h + 1) * U)
                    dve.tensor_reduce(m_real[:, h, :], m_part[:, h, :, :], AX_X, ALU.max).then_inc(real_max, 1)
                elif stage == 1:
                    dve.wait_ge(real_max, 2 * (number + 1) + h + 1)
                    if g < 0:
                        dve.wait_ge(null_copied, 1)
                    dve.tensor_tensor(m_all[:, h, :], m_real[:, h, :],
                                      s_null[:, nb * NB:(nb + 1) * NB, bass.ds(head, 1)].rearrange("p t o -> p (t o)"),
                                      ALU.max).then_inc(head_max, 1)
                else:
                    dve.wait_ge(head_max, 2 * (number + 1) + h + 1)
                    if g >= 0:
                        dve.wait_ge(row_filled, PER_PAIR["row"] * number + NCH * (h + 1))
                    for c in range(NCH):
                        sl = slice(c * BPC, (c + 1) * BPC)
                        dve.tensor_tensor(spread[:, h, sl, :], neg_ident[:].unsqueeze(1).broadcast_to([P, BPC, P]),
                                          m_all[:, h, sl].unsqueeze(2).broadcast_to([P, BPC, P]), ALU.mult
                                          ).then_inc(spread_ready, 1)

            def normalize(g, number, c, rel, stage, bank=None):
                pair = number + rel - ((g + rel) // PAIRS) * PAIRS
                done = NCH * (number + rel) + c + 1
                if stage == 0:
                    dve.wait_ge(den_filled, done)
                    dve.transpose(den_t[:, c, :], misc[:, bank, :]).then_inc(den_turned, 1)
                elif stage == 1:
                    dve.wait_ge(den_turned, done)
                    dve.reciprocal(inv_16[:, c, :], den_t[:, c, 0:CH:32]).then_inc(inv_small, 1)
                elif stage == 2:
                    dve.wait_ge(inv_small, done)
                    dve.tensor_copy(den_t[:, c, :].rearrange("p (j k) -> p j k", k=32),
                                    inv_16[:, c, :].unsqueeze(2).broadcast_to([P, CH // 32, 32])
                                    ).then_inc(inv_wide, 1)
                elif stage == 3:
                    dve.wait_ge(inv_wide, done)
                    dve.transpose(inv[:, c, :], den_t[:, c, :]).then_inc(inv_ready, 1)
                else:
                    dve.wait_ge(inv_ready, done)
                    dve.wait_ge(av_done, TF * (number + rel) + last_of[c])
                    if g == PAIRS and rel == 0:
                        dve.wait_ge(proj_filled, NB)
                    dve.tensor_tensor(
                        heads_out[:, bass.ds(pair, 1), c * CH:(c + 1) * CH].rearrange("p o n -> p (o n)"),
                        o_ps[:, c, :], inv[:, c, :], ALU.mult).then_inc(o_done, 1)

            dve.wait_ge(consts_ready, 3)

            def add_rest(c, bank):
                sl = slice(NB + c * BPC, NB + (c + 1) * BPC)
                dve.wait_ge(proj_copied, B * NB)
                dve.wait_ge(rest_filled, c + 1)
                dve.tensor_tensor(attn[:, sl, :], attn[:, sl, :], bank.rearrange("p (t d) -> p t d", d=D), ALU.add
                                  ).then_inc(rest_added, 1)
                dve.wait_ge(rest_added, c + 1)
                variances(attn, range(NB + c * BPC, NB + (c + 1) * BPC))

            def read_misc(number, g):
                uses = uses_of(g)
                steps = steps_after(uses)
                for n, (kind, rel, i) in enumerate(uses):
                    if kind == "den":
                        normalize(g, number, i, rel, 0, banks_of(g)[kind, rel, i])
                    elif kind == "q" and g >= 0:
                        low_part(g, number, i)
                    elif kind == "unit":
                        unit(g, number, i)
                    elif kind == "rest":
                        add_rest(0, misc[:, banks_of(g)[kind, rel, i], :])
                    for what, rel2, i2, stage in steps[n]:
                        if what == "den":
                            normalize(g, number, i2, rel2, stage)
                        else:
                            whole_max(g, number, i2, stage)
                    if g == B * PAIRS - 1 and (kind, rel) == ("den", -1):
                        dve.wait_ge(proj_copied, NB)
                        variances(attn, range(NB))
                    if g == B * PAIRS - 1 and (kind, rel) == ("den", 0):
                        add_attention(3, range(NB))

            read_misc(-1, -1)
            dve.wait_ge(gate_turned, 1)
            dve.tensor_copy(gate_t[:], o_ps[:, 0, 0:E]).then_inc(gate_split, 1)
            dve.wait_ge(gate_split, 1)
            dve.tensor_copy(gate_hi[:], gate_t[:]).then_inc(gate_split, 1)
            dve.wait_ge(gate_split, 2)
            dve.tensor_tensor(gate_lo[:], gate_t[:], gate_hi[:].bitcast(F32), ALU.subtract).then_inc(gate_split, 1)

            def body(number, g, b):
                read_misc(number, g)
                if g == B * PAIRS - 1:
                    normalize_tokens(4, xn, x_sb, range(NB))
                    for j in range(NCH):
                        low_tokens(1, j, scores[:, 0, j, :])
                    for stage in range(STAGES + 1):
                        normalize(g, number, 1, 0, stage, 0)

            all_pairs(dve, body)

            def shift_logits():
                dve.wait_ge(logits_filled, B)
                ps = misc[:, 1, 0:NT * E].rearrange("p (t e) -> p t e", e=E)
                link(dve.tensor_reduce(low[:], ps, AX_X, ALU.max))
                dve.tensor_tensor(logits[:], ps, low[:].unsqueeze(2).broadcast_to([P, NT, E]), ALU.subtract
                                  ).then_inc(logits_copied, 1)

            def gate():
                dve.wait_ge(exp_done, 1)
                link(dve.tensor_reduce(low[:], rest[:], AX_X, ALU.add))
                link(dve.reciprocal(low[:], low[:]))
                link(dve.tensor_tensor(comb[:], rest[:], low[:].unsqueeze(2).broadcast_to([P, NT, E]), ALU.mult))
                for t in range(NT):
                    done = dve.max(top[:, t, :], comb[:, t, :])
                link(done)

            def choose_experts():
                link(dve.memset(top[:, :, 2:8], -1.0))
                for t in range(NT):
                    done = dve.match_replace(rest[:, t, :], top[:, t, :], comb[:, t, :], 0.0)
                link(done)
                link(dve.tensor_tensor(comb[:], comb[:], rest[:], ALU.subtract))

            def products(number, s, j):
                for i, (_, rows_) in enumerate(pieces_of(s)):
                    n = j * len(pieces_of(s)) + i
                    at = units_before(number) + n
                    dve.wait_ge(silu_done, at + 1)
                    if i == 0 and (s or j >= 2):
                        dve.wait_ge(down_filled, NJ * number + j - 1)
                    dve.tensor_tensor(hidden[0:rows_, j % 2, i, :], gated[0:rows_, n % 2, :],
                                      scores[0:rows_, n % 2, 1, :], ALU.mult).then_inc(hidden_ready, 1)

            def add(number, s, j):
                dve.wait_ge(down_filled, NJ * number + j + 1)
                if s == 0:
                    dve.tensor_copy(attn[:, j * BPC:(j + 1) * BPC, :],
                                    o_ps[:, j % 2, :].rearrange("p (t d) -> p t d", d=D)).then_inc(added, 1)
                    return
                dve.wait_ge(added, NJ * (number - 1) + j + 1)
                for t in range(BPC):
                    tt = j * BPC + t
                    done = dve.scalar_tensor_tensor(out=attn[:, tt, :], in0=o_ps[:, j % 2, t * P:(t + 1) * P],
                                                    scalar=comb[:, tt, bass.ds(number - 1, 1)], in1=attn[:, tt, :],
                                                    op0=ALU.mult, op1=ALU.add)
                done.then_inc(added, 1)

            def finish(j):
                sl = slice(j * BPC, (j + 1) * BPC)
                link(normalize_tokens(9 + j, attn, attn, range(j * BPC, (j + 1) * BPC)))
                dve.tensor_tensor(xn[:, sl, :], x_sb[:, sl, :], attn[:, sl, :], ALU.add).then_inc(result_ready, 1)

            def experts(number, s):
                for j in range(NJ):
                    if s == 0 and j == 1:
                        normalize_tokens(7, xn, x_sb, range(NB, NB + BPC))
                    products(number, s, j)
                    if s == 1 and j == 0:
                        gate()
                    if s == 1 and j == 1:
                        choose_experts()
                    if s == 0 and j == 0:
                        add_rest(1, misc[:, 0, :])
                        add_attention(5, range(NB, NB + BPC))
                    if s == 0 and j == 1:
                        low_tokens(1, 2, misc[:, 0, :])
                        add_attention(6, range(NB + BPC, NT))
                    if s == 0 and j == 2:
                        low_tokens(1, 3, misc[:, 0, :])
                    if s == 0 and j == 3:
                        shift_logits()
                    if j:
                        add(number, s, j - 1)
                    elif s:
                        add(number - 1, s - 1, NJ - 1)
                    if s == 0 and j == 1:
                        normalize_tokens(8, xn, x_sb, range(NB + BPC, NT))
                    if s == E and j:
                        dve.wait_ge(added, NJ * E + j)
                        variances(attn, range((j - 1) * BPC, j * BPC))

            all_experts(dve, experts)
            for j in range(NJ - 2):
                finish(j)
            add(E, E, NJ - 1)
            dve.wait_ge(added, NJ * (E + 1))
            variances(attn, range(NT - BPC, NT))
            for j in range(NJ - 2, NJ):
                finish(j)


_INS = ["L0_attn_x", "L0_attn_Wq", "L0_attn_Wkv", "L0_attn_null_kv", "L0_attn_Wout", "L0_ffn_gate_w", "L0_ffn_w1",
        "L0_ffn_w2", "L0_ffn_w3", "L0_ffn_sw1", "L0_ffn_sw2", "L0_ffn_sw3"]


def kernel(**inputs):
    import ml_dtypes
    import concourse.bacc as bacc
    from concourse.bass_utils import run_bass_kernel_spmd

    nc = bacc.Bacc("TRN2", target_bir_lowering=False, num_devices=1)
    arrays, args = {}, []

    def give(name, a):
        arrays[name] = a
        args.append(nc.dram_tensor(name, a.shape, mybir.dt.from_np(a.dtype), kind="ExternalInput").ap())

    for name in _INS:
        give(f"in_{name}_dram", np.ascontiguousarray(inputs[name]))
    bf16 = ml_dtypes.bfloat16
    give("ident_f", np.eye(P, dtype=np.float32))
    give("ident_b", np.eye(P, dtype=np.float32).astype(bf16))
    key, query = np.arange(P)[:, None], np.arange(-2, P)[None, :]
    give("mask_t", np.where(key > query + 1, MASKED, 0).astype(bf16))
    give("mask_n", np.where(np.arange(P)[None, :] > np.arange(P)[:, None], MASKED, 0).astype(bf16))
    give("mask_fix", np.where(np.eye(2) == 0, MASKED, 0).astype(bf16))
    shape = inputs["L0_attn_x"].shape
    args.append(nc.dram_tensor("out_0_dram", shape, F32, kind="ExternalOutput").ap())
    sandwich_layer(nc, *args)
    r = run_bass_kernel_spmd(nc, [arrays], core_ids=[0])
    return r.results[0]["out_0_dram"]
```
